# Optimizing a Trainium2 kernel written in Bass

```python
import numpy as np
import jax
import jax.numpy as jnp

def _softmax(x, axis=-1):
    return jax.nn.softmax(x, axis=axis)

def _gelu(x):
    return jax.nn.gelu(x, approximate=True)

def _silu(x):
    return jax.nn.silu(x)

def _sigmoid(x):
    return jax.nn.sigmoid(x)

def _layernorm(x, axis=-1, eps=1e-05):
    m = jnp.mean(x, axis=axis, keepdims=True)
    v = jnp.var(x, axis=axis, keepdims=True)
    return (x - m) / jnp.sqrt(v + eps)

def _scatter_add(tgt, idx, src, axis=0):
    return tgt.at[idx].add(src)

def _segment_sum(src, seg, n):
    return jax.ops.segment_sum(src, seg, n)
kernel_name = 'mk_gnn_resnorm_d4_gnn_r32_13a3dc'

def setup_inputs(seed: int=0):
    np.random.seed(seed)
    _w = jnp.asarray

    def _rec_inputs():
        import jax
        import jax.numpy as jnp
        _gk = jax.random.key(seed)
        x = -0.0003713 + 1 * jax.random.normal(jax.random.fold_in(_gk, 1), (3125, 128), jnp.float32)
        _s = jax.random.randint(jax.random.fold_in(_gk, 2), (25000,), 0, 3125, jnp.int32)
        _d = jax.random.randint(jax.random.fold_in(_gk, 3), (25000,), 0, 3125, jnp.int32)
        _loop = jnp.arange(3125, dtype=jnp.int32)
        src = jnp.concatenate([_s, _d, _loop])
        dst = jnp.concatenate([_d, _s, _loop])
        _o = jnp.argsort(dst, stable=True)
        src = src[_o]
        dst = dst[_o]
        edge_attr_32 = 0.000189758 + 1.00013 * jax.random.normal(jax.random.fold_in(_gk, 12), (53125, 32), jnp.float32)
        edge_attr_64 = -9.77346e-05 + 0.999888 * jax.random.normal(jax.random.fold_in(_gk, 13), (53125, 64), jnp.float32)
        node_vec = -0.00396605 + 0.997609 * jax.random.normal(jax.random.fold_in(_gk, 15), (3125,), jnp.float32)
        return (x, src, dst, edge_attr_32, edge_attr_64, node_vec)
    x, src, dst, edge_attr_32, edge_attr_64, node_vec = _rec_inputs()

    def _L0_gnn_setup():
        import jax, jax.numpy as jnp
        import numpy as np
        N = 3125
        E = 50000
        H = 8
        C = 16
        DIM = 128
        EDGE_DIM = 32
        key = jax.random.key(seed)
        ks = jax.random.split(key, 7)
        s = 1.0 / np.sqrt(DIM)
        return {'x': jax.random.normal(ks[0], (N, DIM), dtype=jnp.float32), 'edge_index': jax.random.randint(ks[1], (2, E), 0, N, dtype=jnp.int32), 'edge_attr': jax.random.normal(ks[2], (E, EDGE_DIM), dtype=jnp.float32), 'Wq': jax.random.normal(ks[3], (H * C, DIM), dtype=jnp.float32) * s, 'Wk': jax.random.normal(ks[4], (H * C, DIM), dtype=jnp.float32) * s, 'Wv': jax.random.normal(ks[5], (H * C, DIM), dtype=jnp.float32) * s, 'We': jax.random.normal(ks[6], (H, EDGE_DIM), dtype=jnp.float32) * (1.0 / np.sqrt(EDGE_DIM))}
    _L0_gnn_all = _L0_gnn_setup()
    _L0_gnn_in = {k: v for k, v in _L0_gnn_all.items() if k in ('Wq', 'Wk', 'Wv', 'We')}
    del _L0_gnn_all

    def _L1_gnn_setup():
        import jax, jax.numpy as jnp
        import numpy as np
        N = 3125
        E = 50000
        F = 128
        UNITS = 128
        key = jax.random.key(seed)
        k1, k2, k3, k4 = jax.random.split(key, 4)
        node_states = jax.random.normal(k1, (N, F), dtype=jnp.float32)
        src = jax.random.randint(k2, (E,), 0, N)
        dst = jax.random.randint(k3, (E,), 0, N)
        kernel = jax.random.normal(k4, (F, UNITS), dtype=jnp.float32) / np.float32(np.sqrt(F))
        bias = jnp.zeros((UNITS,), dtype=jnp.float32)
        return {'node_states': node_states, 'src': src, 'dst': dst, 'kernel': kernel, 'bias': bias}
    _L1_gnn_all = _L1_gnn_setup()
    _L1_gnn_in = {k: v for k, v in _L1_gnn_all.items() if k in ('kernel', 'bias')}
    del _L1_gnn_all

    def _L2_gnn_setup():
        import jax, jax.numpy as jnp
        import numpy as np
        NEG_SLOPE = 0.05

        def leaky(x):
            return jnp.where(x >= 0, x, NEG_SLOPE * x)

        def segment_softmax(e, seg, num_segments):
            m = jax.ops.segment_max(e, seg, num_segments=num_segments)
            ex = jnp.exp(e - m[seg])
            s = jax.ops.segment_sum(ex, seg, num_segments=num_segments)
            return ex / s[seg]

        def scatter_mean(vals, seg, num_segments):
            tot = jax.ops.segment_sum(vals, seg, num_segments=num_segments)
            cnt = jax.ops.segment_sum(jnp.ones((vals.shape[0],), vals.dtype), seg, num_segments=num_segments)
            return tot / jnp.maximum(cnt, 1.0)[:, None]
        key = jax.random.key(seed)
        ks = jax.random.split(key, 7)
        N, E, Fn, Fe, D = (50000, 25000, 128, 64, 64)
        return {'x': jax.random.normal(ks[0], (N, Fn), jnp.float32), 'edge_attr': jax.random.normal(ks[1], (E, Fe), jnp.float32), 'edge_index': jax.random.randint(ks[2], (2, E), 0, N, jnp.int64), 'W_node': jax.random.normal(ks[3], (D, Fn), jnp.float32) * 0.05, 'W_edge': jax.random.normal(ks[4], (D, Fe), jnp.float32) * 0.05, 'a_node': jax.random.normal(ks[5], (2 * D,), jnp.float32) * 0.05, 'a_edge': jax.random.normal(ks[6], (2 * D,), jnp.float32) * 0.05}
    _L2_gnn_all = _L2_gnn_setup()
    _L2_gnn_in = {k: v for k, v in _L2_gnn_all.items() if k in ('W_node', 'W_edge', 'a_node', 'a_edge')}
    del _L2_gnn_all

    def _L3_gnn_setup():
        import jax, jax.numpy as jnp
        import numpy as np
        N = 3125
        E = 50000
        D = 128
        NEG_SLOPE = 0.2

        def _edge_softmax(logits, dst, n):
            m = jax.ops.segment_max(logits, dst, num_segments=n)
            ex = jnp.exp(logits - m[dst])
            denom = jax.ops.segment_sum(ex, dst, num_segments=n)
            return ex / denom[dst]
        key = jax.random.key(seed)
        ks = jax.random.split(key, 8)
        s = 1.0 / np.sqrt(D)
        return {'feat': jax.random.normal(ks[0], (N, D), dtype=jnp.float32), 'simi_weight': jax.random.normal(ks[1], (N,), dtype=jnp.float32), 'W_homo': jax.random.normal(ks[2], (D, D), dtype=jnp.float32) * s, 'b_homo': jnp.zeros((D,), dtype=jnp.float32), 'W_hete': jax.random.normal(ks[3], (D, D), dtype=jnp.float32) * s, 'b_hete': jnp.zeros((D,), dtype=jnp.float32), 'W_self': jax.random.normal(ks[4], (D, D), dtype=jnp.float32) * s, 'b_self': jnp.zeros((D,), dtype=jnp.float32), 'src_idx': jax.random.randint(ks[5], (E,), 0, N, dtype=jnp.int32), 'dst_idx': jax.random.randint(ks[6], (E,), 0, N, dtype=jnp.int32)}
    _L3_gnn_all = _L3_gnn_setup()
    _L3_gnn_in = {k: v for k, v in _L3_gnn_all.items() if k in ('W_homo', 'b_homo', 'W_hete', 'b_hete', 'W_self', 'b_self')}
    del _L3_gnn_all
    return {'x': x, 'src': src, 'dst': dst, 'edge_attr_32': edge_attr_32, 'edge_attr_64': edge_attr_64, 'node_vec': node_vec, 'L0_gnn_Wq': _L0_gnn_in['Wq'], 'L0_gnn_Wk': _L0_gnn_in['Wk'], 'L0_gnn_Wv': _L0_gnn_in['Wv'], 'L0_gnn_We': _L0_gnn_in['We'], 'L1_gnn_kernel': _L1_gnn_in['kernel'], 'L1_gnn_bias': _L1_gnn_in['bias'], 'L2_gnn_W_node': _L2_gnn_in['W_node'], 'L2_gnn_W_edge': _L2_gnn_in['W_edge'], 'L2_gnn_a_node': _L2_gnn_in['a_node'], 'L2_gnn_a_edge': _L2_gnn_in['a_edge'], 'L3_gnn_W_homo': _L3_gnn_in['W_homo'], 'L3_gnn_b_homo': _L3_gnn_in['b_homo'], 'L3_gnn_W_hete': _L3_gnn_in['W_hete'], 'L3_gnn_b_hete': _L3_gnn_in['b_hete'], 'L3_gnn_W_self': _L3_gnn_in['W_self'], 'L3_gnn_b_self': _L3_gnn_in['b_self']}

def reference(x, src, dst, edge_attr_32, edge_attr_64, node_vec, L0_gnn_Wq, L0_gnn_Wk, L0_gnn_Wv, L0_gnn_We, L1_gnn_kernel, L1_gnn_bias, L2_gnn_W_node, L2_gnn_W_edge, L2_gnn_a_node, L2_gnn_a_edge, L3_gnn_W_homo, L3_gnn_b_homo, L3_gnn_W_hete, L3_gnn_b_hete, L3_gnn_W_self, L3_gnn_b_self):
    import jax
    import jax.numpy as jnp

    def _L0_gnn_ref(x, edge_index, edge_attr, Wq, Wk, Wv, We):
        import jax, jax.numpy as jnp
        import numpy as np
        N = 3125
        E = 50000
        H = 8
        C = 16
        DIM = 128
        EDGE_DIM = 32
        q = (x @ Wq.T).reshape(N, H, C)
        k = (x @ Wk.T).reshape(N, H, C)
        v = (x @ Wv.T).reshape(N, H, C)
        src, dst = (edge_index[0], edge_index[1])
        edge_bias = edge_attr @ We.T
        scores = jnp.einsum('ehc,ehc->eh', q[dst], k[src]) / np.sqrt(C) + edge_bias
        seg_max = jax.ops.segment_max(scores, dst, num_segments=N)
        ex = jnp.exp(scores - seg_max[dst])
        denom = jax.ops.segment_sum(ex, dst, num_segments=N)
        alpha = ex / denom[dst]
        msgs = v[src] * alpha[:, :, None]
        out = jax.ops.segment_sum(msgs, dst, num_segments=N)
        return out.reshape(N, H * C)

    def _L1_gnn_ref(node_states, src, dst, kernel, bias):
        import jax, jax.numpy as jnp
        import numpy as np
        N = 3125
        E = 50000
        F = 128
        UNITS = 128
        n = node_states.shape[0]
        ones = jnp.ones(src.shape, dtype=node_states.dtype)
        deg = jax.ops.segment_sum(ones, src, num_segments=n)
        dinv = jnp.where(deg > 0, 1.0 / jnp.sqrt(jnp.maximum(deg, 1.0)), 0.0)
        xw = node_states @ kernel
        coef = (dinv[src] * dinv[dst])[:, None]
        msg = xw[dst] * coef
        out = jax.ops.segment_sum(msg, src, num_segments=n)
        out = out + bias
        return jax.nn.relu(out)

    def _L2_gnn_ref(x, edge_attr, edge_index, W_node, W_edge, a_node, a_edge):
        import jax, jax.numpy as jnp
        import numpy as np
        NEG_SLOPE = 0.05

        def leaky(x):
            return jnp.where(x >= 0, x, NEG_SLOPE * x)

        def segment_softmax(e, seg, num_segments):
            m = jax.ops.segment_max(e, seg, num_segments=num_segments)
            ex = jnp.exp(e - m[seg])
            s = jax.ops.segment_sum(ex, seg, num_segments=num_segments)
            return ex / s[seg]

        def scatter_mean(vals, seg, num_segments):
            tot = jax.ops.segment_sum(vals, seg, num_segments=num_segments)
            cnt = jax.ops.segment_sum(jnp.ones((vals.shape[0],), vals.dtype), seg, num_segments=num_segments)
            return tot / jnp.maximum(cnt, 1.0)[:, None]
        N = x.shape[0]
        E = edge_index.shape[1]
        D = W_node.shape[0]
        h = x @ W_node.T
        g = edge_attr @ W_edge.T
        loops = jnp.arange(N, dtype=edge_index.dtype)
        i_idx = jnp.concatenate([edge_index[0], loops])
        j_idx = jnp.concatenate([edge_index[1], loops])
        hi = h @ a_node[:D]
        hj = h @ a_node[D:]
        e_n = leaky(hi[i_idx] + hj[j_idx])
        alpha_n = segment_softmax(e_n, i_idx, N)
        x_from_nodes = scatter_mean(alpha_n[:, None] * h[j_idx], i_idx, N)
        i_idx_e = jnp.concatenate([edge_index[0], edge_index[1]])
        g2 = jnp.concatenate([g, g], axis=0)
        he = h @ a_edge[:D]
        ge = g @ a_edge[D:]
        ge2 = jnp.concatenate([ge, ge])
        e_e = leaky(he[i_idx_e] + ge2)
        alpha_e = segment_softmax(e_e, i_idx_e, N)
        x_from_edges = scatter_mean(alpha_e[:, None] * g2, i_idx_e, N)
        return jnp.concatenate([leaky(x_from_nodes), leaky(x_from_edges)], axis=-1)

    def _L3_gnn_ref(feat, simi_weight, W_homo, b_homo, W_hete, b_hete, W_self, b_self, src_idx, dst_idx):
        import jax, jax.numpy as jnp
        import numpy as np
        N = 3125
        E = 50000
        D = 128
        NEG_SLOPE = 0.2

        def _edge_softmax(logits, dst, n):
            m = jax.ops.segment_max(logits, dst, num_segments=n)
            ex = jnp.exp(logits - m[dst])
            denom = jax.ops.segment_sum(ex, dst, num_segments=n)
            return ex / denom[dst]
        n = feat.shape[0]
        e = simi_weight[src_idx]
        lrelu = lambda x: jnp.where(x > 0, x, NEG_SLOPE * x)
        a_homo = _edge_softmax(lrelu(e), dst_idx, n)
        a_hete = _edge_softmax(lrelu(-e), dst_idx, n)
        mask = e > 0
        w_homo = jnp.where(mask, a_homo, 0.0)
        w_hete = jnp.where(mask, 0.0, a_hete)
        fsrc = feat[src_idx]
        neigh_homo = jax.ops.segment_sum(fsrc * w_homo[:, None], dst_idx, num_segments=n)
        neigh_hete = jax.ops.segment_sum(fsrc * w_hete[:, None], dst_idx, num_segments=n)
        h_neigh = neigh_homo @ W_homo + b_homo + (neigh_hete @ W_hete + b_hete)
        return feat @ W_self + b_self + h_neigh
    edge_index = jnp.stack([src, dst])
    x = _layernorm(x + _L0_gnn_ref(x, edge_index, edge_attr_32, L0_gnn_Wq, L0_gnn_Wk, L0_gnn_Wv, L0_gnn_We), axis=-1)
    x = _layernorm(x + _L1_gnn_ref(x, src, dst, L1_gnn_kernel, L1_gnn_bias), axis=-1)
    x = _layernorm(x + _L2_gnn_ref(x, edge_attr_64, edge_index, L2_gnn_W_node, L2_gnn_W_edge, L2_gnn_a_node, L2_gnn_a_edge), axis=-1)
    x = _layernorm(x + _L3_gnn_ref(x, node_vec, L3_gnn_W_homo, L3_gnn_b_homo, L3_gnn_W_hete, L3_gnn_b_hete, L3_gnn_W_self, L3_gnn_b_self, src, dst), axis=-1)
    return x

_drawn_inputs = setup_inputs


def setup_inputs(seed=0):
    import zlib

    import numpy as np

    out = dict(_drawn_inputs(seed))
    spreads = {'L1_gnn_bias': (0.0, 0.1),
     'L3_gnn_b_homo': (0.0, 0.1),
     'L3_gnn_b_hete': (0.0, 0.1),
     'L3_gnn_b_self': (0.0, 0.1)}
    factors = {'edge_attr_64': 8.0,
     'L2_gnn_W_node': 8.0,
     'L2_gnn_W_edge': 8.0,
     'L2_gnn_a_node': 8.0,
     'L2_gnn_a_edge': 8.0}
    for name, (base, spread) in spreads.items():
        noise = np.random.default_rng([zlib.crc32(name.encode()), seed]).standard_normal(out[name].shape)
        drawn = base * np.exp(spread * noise) if base else spread * noise
        out[name] = jnp.asarray(drawn.astype(out[name].dtype))
    for name, factor in factors.items():
        out[name] = (out[name] * factor).astype(out[name].dtype)
    return out
```

```python
from contextlib import ExitStack

import concourse.bass as bass
from concourse import mybir

F32 = mybir.dt.float32
I32 = mybir.dt.int32
BF16 = mybir.dt.bfloat16
F16 = mybir.dt.float16
ALU = mybir.AluOpType
ACT = mybir.ActivationFunctionType
AX_X = mybir.AxisListType.X
DVE_ONLY = (mybir.EngineType.DVE,)
PE_ONLY = (mybir.EngineType.PE,)

P = 128
N = 3125
D = 128
E = 53125
H, C = 8, 16
FE32, FE64 = 32, 64
NB = -(-N // P)
NPAD = NB * P
ET = -(-E // (8 * P)) * 8
EROWS = P * ET
T = -(-(E // P + NB) // 8) * 8
NH = NB + 1
ROW = FE64 + FE32 + 2
C_SRC, C_DST = FE64 + FE32, FE64 + FE32 + 1
KVW = 2 * D + 1
G = 4
SR = T // 4
SL = 4 * P
BIG = 3.0e38
NOWHERE = 60000.0
EPS = 1e-5
WN = 68


def wait(eng, sem, value):
    if isinstance(value, int) and value <= 0:
        return
    eng.wait_ge(sem, value)


def hold(eng, sem, value, passed):
    if isinstance(value, int):
        wait(eng, sem, value)
        return
    eng.wait_ge(sem, value)
    eng.sem_inc(passed, 1)


def loop(eng, count, body, last_too=False):
    body(0)
    with eng.Fori(1, count - 1 if last_too else count) as i:
        body(i)
    if last_too:
        body(count - 1)


class Chain:

    def __init__(self, eng, sem):
        self.eng, self.sem, self.per, self.k, self.i, self.base = eng, sem, 0, 0, 0, 0

    def start(self, i):
        if not (isinstance(i, int) and i == 0) and not self.per:
            self.per = self.k
        self.i, self.k = i, 0

    def link(self, ins):
        ins.then_inc(self.sem, 1)
        self.k += 1
        at = self.i * self.per + self.k if self.per else self.k
        self.eng.wait_ge(self.sem, at)


def gnn_program(nc, x, keys, edge_pair, edge_attr, node_vec, Wqkv, WeT, L1_kernel, L1_bias, W_node,
                W_nodeT, W_edge, W_edgeT, a_node, a_edge, L3_W, L3_b, out):
    ctx = ExitStack()
    with ctx:
        def sb(name, shape, dt=F32):
            return ctx.enter_context(nc.sbuf_tensor(name, shape, dt))

        stage_sems = []

        def lasting_sem(name):
            return ctx.enter_context(nc.semaphore(name))

        def sem(name):
            stage_sems.append(nc.alloc_semaphore(name=name))
            return stage_sems[-1]

        def recycle():
            with nc.Block() as block:
                @block.gpsimd
                def _(g):
                    nc.clear_and_free_semaphores(stage_sems)
                    for s in passed.values():
                        g.sem_clear(s)
            stage_sems.clear()

        def dram(name, shape):
            return nc.dram_tensor(name, shape, F32).ap()

        ps = [ctx.enter_context(nc.psum_tensor(f"ps{i}", [P, 512], F32)) for i in range(8)]

        edge_table = dram("edge_table", (E, ROW))
        kv_table = dram("kv_table", (NPAD, KVW))
        y_table = dram("y_table", (NPAD, D))
        n_table = dram("n_table", (NPAD, WN))
        x_table = dram("x_table", (NPAD, D))
        v_rows = dram("v_rows", (T, P, D))
        a_rows = {"dst": dram("a_rows_dst", (T, P, FE64)), "src": dram("a_rows_src", (T, P, FE64))}
        h_rows = dram("h_rows", (T, P, FE64))

        diff = sb("diff", [P, P])
        ident = sb("ident", [P, P])
        ident16 = sb("ident16", [P, P], BF16)
        iota0 = sb("iota0", [P, P])
        iota0h = sb("iota0h", [P, P], BF16)
        iota1 = sb("iota1", [P, P])
        iotaT = sb("iotaT", [P, T])
        iotaTh = sb("iotaTh", [P, T], F16)
        ones = sb("ones", [P, P])
        after = sb("after", [P, P])
        upto = sb("upto", [P, P])
        down1 = sb("down1", [P, P])
        up1 = sb("up1", [P, P])

        wqkv = sb("wqkv", [P, 3 * D])
        we_bd = sb("we_bd", [P, G * H])
        w1 = sb("w1", [P, D])
        b1 = sb("b1", [P, D])
        wn = sb("wn", [P, WN])
        wnode = sb("wnode", [FE64, D])
        wedge = sb("wedge", [FE64, FE64])
        wedgeT = sb("wedgeT", [FE64, FE64])
        avec = sb("avec", [FE64, 4])
        a_rep = sb("a_rep", [FE64, P])
        wge = sb("wge", [P, FE64])
        w3 = sb("w3", [P, 3, D])
        b3 = sb("b3", [P, 3, D])

        xs = sb("xs", [P, NB, D])
        nv = sb("nv", [P, NB])
        acc = sb("acc", [P, NB * (2 * D + 2)])
        qs = sb("qs", [P, NB, D])
        node_vals = sb("node_vals", [P, NB, 4])
        cnt = {o: sb(f"cnt_{o}", [P, NH]) for o in ("dst", "src")}
        gmax = {o: sb(f"gmax_{o}", [P, NB]) for o in ("dst", "src")}
        small = sb("small", [P, 8, NH])
        smalli = sb("smalli", [P, NH], I32)
        xt = sb("xt", [P, G, P])
        nout = sb("nout", [P, G, KVW])

        eidx = {o: sb(f"eidx_{o}", [P, T], I32) for o in ("dst", "src")}
        valid = {o: sb(f"valid_{o}", [P, T]) for o in ("dst", "src")}
        lo1 = {o: sb(f"lo1_{o}", [P, T]) for o in ("dst", "src")}
        node = {o: sb(f"node_{o}", [P, T]) for o in ("dst", "src")}
        other = {o: sb(f"other_{o}", [P, T], I32) for o in ("dst", "src")}
        bid = {o: sb(f"bid_{o}", [1, T], I32) for o in ("dst", "src")}
        is_last = {o: sb(f"last_{o}", [P, T]) for o in ("dst", "src")}
        ge = {o: sb(f"ge_{o}", [P, T]) for o in ("dst", "src")}
        exe = {o: sb(f"exe_{o}", [P, T]) for o in ("dst", "src")}
        gm_slot = sb("gm_slot", [P, T])
        KD = H + 2
        S = sb("S", [P, T, KD])
        selfv = S[:, :, 0:4]
        slot_tmp = [sb(f"slot_tmp{i}", [P, T]) for i in range(4)]

        work = sb("work", [P, NH * (ET + 1)])
        table = work[:, :].rearrange("p (h t) -> p h t", h=NH)
        wide = work[:, 0:NB * D].rearrange("p (b d) -> p b d", b=NB)
        scan = [work[0:SR, k * SL:(k + 1) * SL] for k in range(6)]
        edge_cols = [S[:, :, :].rearrange("p t c -> p (t c)")[:, k * ET:(k + 1) * ET] for k in range(8)]
        key = {"lo": edge_cols[0], "hi": edge_cols[1]}
        keyi, keyt, number = (edge_cols[k].bitcast(I32) for k in (2, 3, 4))
        pos, num_hi, num_lo = edge_cols[5:8]
        colsA = sb("colsA", [P, 4, 8])
        rowsA = sb("rowsA", [8, 4, P])

        oh = [sb(f"oh{h}", [P, G, P]) for h in range(2)]
        rhs = [sb(f"rhs{h}", [P, G, 2 * D + 2]) for h in range(2)]
        flat_rhs = [r[:, :, :].rearrange("p g c -> p (g c)") for r in rhs]
        ohT = [r[:, 0:G * P].rearrange("p (g n) -> p g n", g=G) for r in flat_rhs]
        oh16, same = ([r[:, at:at + G * P // 2].bitcast(BF16).rearrange("p (g n) -> p g n", g=G) for r in flat_rhs]
                      for at in (G * P, 3 * G * P // 2))
        hi16 = [sb(f"hi16{h}", [P, G, NH], BF16) for h in range(2)]
        prod = [sb(f"prod{h}", [P, G, P]) for h in range(2)]
        big16 = [acc[:, h * G * T // 2:(h + 1) * G * T // 2].bitcast(BF16).rearrange("p (g t) -> p g t", g=G)
                 for h in range(2)]
        stage = [sb(f"stage{h}", [P, G], I32) for h in range(2)]
        erow = [sb(f"erow{h}", [P, G, ROW]) for h in range(2)]
        arow = [e[:, :, 0:FE64] for e in erow]
        grow = [sb(f"grow{h}", [P, G, KVW]) for h in range(2)]
        efeat = [sb(f"efeat{h}", [P, G * FE32]) for h in range(2)]
        tiny = [sb(f"tiny{h}", [P, 1, G * H]) for h in range(2)]
        tinyi = [sb(f"tinyi{h}", [P, G], I32) for h in range(2)]

        passed = {e: lasting_sem(f"passed_{e}") for e in ("act", "pool", "dve", "pe")}
        landed = [lasting_sem(f"gather_landed{i}") for i in range(2 * G)]
        rounds = [0]

        def blk(kind):
            return nc.Block()

        s_w, s_c, s_cd, s_wp = sem("weights_loaded"), sem("iotas_ready"), sem("consts_chain"), sem("wfold_done")
        s_t = sem("edge_table_written")
        s_xz = sem("x_cleared")
        with nc.Block() as block:
            @block.sync
            def _(sp):
                sp.wait_ge(s_xz, 1)
                full = (NB - 1) * P
                sp.dma_start(xs[:, 0:NB - 1, :], x[0:full, :].rearrange("(b p) d -> p b d", p=P)).then_inc(s_w, 16)
                sp.dma_start(xs[0:N - full, NB - 1, :], x[full:N, :]).then_inc(s_w, 16)
                with nc.allow_non_contiguous_dma(reason="node_vec into node layout"):
                    sp.dma_start(nv[:, 0:NB - 1], node_vec[0:full].rearrange("(b p) -> p b", p=P)).then_inc(s_w, 16)
                    sp.dma_start(nv[0:N - full, NB - 1:NB], node_vec[full:N].rearrange("(p o) -> p o", o=1)).then_inc(s_w, 16)
                sp.dma_start(wqkv[:, :], Wqkv).then_inc(s_w, 16)
                for j in range(G):
                    sp.dma_start(we_bd[j * FE32:(j + 1) * FE32, j * H:(j + 1) * H], WeT).then_inc(s_w, 16)
                sp.dma_start(w1[:, :], L1_kernel).then_inc(s_w, 16)
                sp.dma_start(b1[:, :], L1_bias[None, :].to_broadcast([P, D])).then_inc(s_w, 16)
                sp.dma_start(wnode[:, :], W_node).then_inc(s_w, 16)
                sp.dma_start(wn[:, 0:FE64], W_nodeT).then_inc(s_w, 16)
                sp.dma_start(wedge[:, :], W_edge).then_inc(s_w, 16)
                sp.dma_start(wedgeT[:, :], W_edgeT).then_inc(s_w, 16)
                with nc.allow_non_contiguous_dma(reason="attention vectors as columns"):
                    sp.dma_start(avec[:, 0:2], a_node.rearrange("(a d) -> d a", a=2)).then_inc(s_w, 16)
                    sp.dma_start(avec[:, 2:4], a_edge.rearrange("(a d) -> d a", a=2)).then_inc(s_w, 16)
                sp.dma_start(w3[:, :, :], L3_W.rearrange("m p d -> p m d")).then_inc(s_w, 16)
                for j in range(3):
                    sp.dma_start(b3[:, j, :], L3_b[j:j + 1, :].to_broadcast([P, D])).then_inc(s_w, 16)
                sp.wait_ge(s_w, 16 * 21)

            @block.scalar
            def _(act):
                act.dma_start(edge_table[:, 0:FE64 + FE32], edge_attr).then_inc(s_t, 16)
                act.dma_start(edge_table[:, C_SRC:C_SRC + 2].bitcast(I32), edge_pair).then_inc(s_t, 16)

            @block.gpsimd
            def _(g):
                nc.gpsimd.iota(diff[:, :], [[1, P]], base=0, channel_multiplier=-1,
                               allow_small_or_imprecise_dtypes=True).then_inc(s_c, 1)
                nc.gpsimd.iota(iota0[:, :], [[1, P]], base=0, channel_multiplier=0,
                               allow_small_or_imprecise_dtypes=True).then_inc(s_c, 1)
                nc.gpsimd.iota(iotaT[:, :], [[1, T]], base=0, channel_multiplier=0,
                               allow_small_or_imprecise_dtypes=True).then_inc(s_c, 1)
                nc.gpsimd.iota(number[:, :], [[1, ET]], base=1, channel_multiplier=ET).then_inc(s_c, 1)

            @block.vector
            def _(v):
                nc.vector.memset(we_bd[:, :], 0.0)
                nc.vector.memset(nv[:, :], 0.0)
                nc.vector.memset(wn[:, :], 0.0)
                nc.vector.memset(xs[:, :, :], 0.0).then_inc(s_xz, 1)
                v.wait_ge(s_c, 4)
                nc.vector.memset(ones[:, :], 1.0)
                for to, op, at in ((ident, ALU.is_equal, 0.0), (ident16, ALU.is_equal, 0.0), (after, ALU.is_gt, 0.0),
                                   (upto, ALU.is_ge, 0.0), (down1, ALU.is_equal, 1.0), (up1, ALU.is_equal, -1.0)):
                    nc.vector.tensor_scalar(to[:, :], diff[:, :], at, None, op)
                nc.vector.tensor_scalar(iota0h[:, :], iota0[:, :], 0.0, None, ALU.add)
                nc.vector.tensor_scalar(iota1[:, :], iota0[:, :], 1.0, None, ALU.add)
                nc.vector.tensor_scalar(iotaTh[:, :], iotaT[:, :], 0.0, None, ALU.add)
                ch = Chain(v, s_cd)
                ch.link(nc.vector.tensor_scalar(keyt[:, :], number[:, :], 8, None, ALU.arith_shift_right))
                nc.vector.tensor_copy(num_hi[:, :], keyt[:, :])
                ch.link(nc.vector.tensor_scalar(keyi[:, :], number[:, :], 255, None, ALU.bitwise_and))
                nc.vector.tensor_copy(num_lo[:, :], keyi[:, :])
                v.wait_ge(s_w, 16 * 21)
                ch.link(nc.vector.tensor_copy(a_rep[:, :], avec[:, 3:4].to_broadcast([FE64, P])))
                v.wait_ge(s_wp, 2)
                nc.vector.tensor_copy(wge[:, :], ps[0][:, 0:FE64])
                nc.vector.tensor_copy(wn[:, 64:65], ps[1][:, 1:2])
                nc.vector.tensor_copy(wn[:, 65:66], ps[1][:, 0:1])
                nc.vector.tensor_copy(wn[:, 66:67], ps[1][:, 2:3])

            @block.tensor
            def _(pe):
                pe.wait_ge(s_cd, 3)
                nc.tensor.matmul(ps[0][:, 0:FE64], a_rep[:, :], wedge[:, :], start=True, stop=True).then_inc(s_wp, 1)
                nc.tensor.matmul(ps[1][:, 0:4], wnode[:, :], avec[:, :], start=True, stop=True).then_inc(s_wp, 1)

        def sort(o, which):
            s_k, s_ch = sem(f"{o}_keys_loaded"), sem(f"{o}_key_chain")
            s_oh, s_hd, s_hc = sem(f"{o}_hist_onehots"), sem(f"{o}_hist_done"), sem(f"{o}_hist_copied")
            with nc.Block() as block:
                @block.sync
                def _(sp):
                    sp.dma_start(keyi[:, :], keys[which]).then_inc(s_k, 16)

                @block.vector
                def _(v):
                    ch = Chain(v, s_ch)
                    v.wait_ge(s_k, 16)
                    ch.link(nc.vector.tensor_scalar(keyt[:, :], keyi[:, :], 7, None, ALU.arith_shift_right))
                    ch.link(nc.vector.tensor_copy(key["hi"][:, :], keyt[:, :]))
                    ch.link(nc.vector.tensor_scalar(keyt[:, :], keyi[:, :], P - 1, None, ALU.bitwise_and))
                    ch.link(nc.vector.tensor_copy(key["lo"][:, :], keyt[:, :]))
                    nc.vector.memset(table[:, :, 0:1], 0.0)

                    def body(i):
                        for h in range(2):
                            t0 = i * (2 * G) + h * G
                            wait(v, s_hd, i * 2 + (h - 1))
                            nc.vector.tensor_tensor(oh16[h][:, :, :], iota0[:, None, :].to_broadcast([P, G, P]),
                                                    key["lo"][:, bass.ds(t0, G)].to_broadcast([P, G, P]), ALU.is_equal)
                            nc.vector.tensor_tensor(hi16[h][:, :, :], iota0[:, None, 0:NH].to_broadcast([P, G, NH]),
                                                    key["hi"][:, bass.ds(t0, G)].to_broadcast([P, G, NH]),
                                                    ALU.is_equal).then_inc(s_oh, 1)
                    loop(v, ET // (2 * G), body)

                @block.tensor
                def _(pe):
                    def body(i):
                        for h in range(2):
                            pe.wait_ge(s_oh, i * 2 + (h + 1))
                            wait(pe, s_hc, i * 2 + (h - 1))
                            for j in range(G):
                                last = nc.tensor.matmul(ps[h][:, j * NH:(j + 1) * NH], oh16[h][:, j, :],
                                                        hi16[h][:, j, :], start=True, stop=True)
                            last.then_inc(s_hd, 1)
                    loop(pe, ET // (2 * G), body)

                @block.scalar
                def _(act):
                    def body(i):
                        for h in range(2):
                            hold(act, s_hd, i * 2 + (h + 1), passed["act"])
                            nc.scalar.copy(table[:, :, bass.ds(i * (2 * G) + (h * G + 1), G)],
                                           ps[h][:, 0:G * NH].rearrange("p (g n) -> p n g", g=G)).then_inc(s_hc, 1)
                    loop(act, ET // (2 * G), body)

            s_v, s_p = sem(f"{o}_starts_chain"), sem(f"{o}_starts_products")
            total, tiles, ends, start, base = (small[:, k, :] for k in range(5))
            endc = small[0:NB, 5, 0:2]
            with nc.Block() as block:
                @block.vector
                def _(v):
                    ch = Chain(v, s_v)
                    ch.link(nc.vector.tensor_reduce(out=cnt[o][:, :], in_=table[:, :, 1:ET + 1], axis=AX_X, op=ALU.add))
                    v.wait_ge(s_p, 3)
                    ch.link(nc.vector.tensor_scalar(total, ps[0][:, 0:NH], float(P - 1), None, ALU.add))
                    ch.link(nc.vector.tensor_copy(smalli[:, :], total))
                    ch.link(nc.vector.tensor_scalar(smalli[:, :], smalli[:, :], 7, None, ALU.arith_shift_right))
                    ch.link(nc.vector.tensor_copy(tiles, smalli[:, :]))
                    ch.link(nc.vector.tensor_tensor_scan(ends, ones[:, 0:NH], tiles, 0.0, ALU.mult, ALU.add))
                    ch.link(nc.vector.tensor_tensor(start, ends, tiles, ALU.subtract))
                    ch.link(nc.vector.scalar_tensor_tensor(out=base, in0=start, scalar=float(P), in1=ps[1][:, 0:NH],
                                                           op0=ALU.mult, op1=ALU.add))
                    ch.link(nc.vector.memset(small[:, 4, NB:NH], NOWHERE))
                    ch.link(nc.vector.tensor_scalar(endc[:, 0:1], ps[2][0:NB, 0:1], float(P - 1), None, ALU.add))
                    ch.link(nc.vector.tensor_copy(smalli[0:NB, 0:1], endc[:, 0:1]))
                    ch.link(nc.vector.tensor_scalar(smalli[0:NB, 0:1], smalli[0:NB, 0:1], 7, None, ALU.arith_shift_right))
                    ch.link(nc.vector.tensor_copy(endc[:, 0:1], smalli[0:NB, 0:1]))
                    v.wait_ge(s_p, 4)
                    ch.link(nc.vector.tensor_copy(endc[:, 1:2], ps[3][0:NB, 0:1]))
                    ch.link(nc.vector.tensor_scalar(slot_tmp[0][0:NB, :], iotaT[0:NB, :], endc[:, 1:2], None, ALU.is_ge))
                    v.wait_ge(s_p, 5)
                    ch.link(nc.vector.tensor_scalar(bid[o][0:1, :], ps[4][0:1, 0:T], float(NB - 1), None, ALU.min))
                    for b in range(NH):
                        nc.vector.tensor_tensor_scan(table[:, b, :], ones[:, 0:1].to_broadcast([P, ET + 1]), table[:, b, :],
                                                     small[:, 4, b:b + 1], ALU.mult, ALU.add)

                @block.tensor
                def _(pe):
                    pe.wait_ge(s_v, 1)
                    nc.tensor.matmul(ps[0][:, 0:NH], ones[:, :], cnt[o][:, :], start=True, stop=True).then_inc(s_p, 1)
                    nc.tensor.matmul(ps[1][:, 0:NH], after[:, :], cnt[o][:, :], start=True, stop=True).then_inc(s_p, 1)
                    nc.tensor.matmul(ps[2][0:NB, 0:1], cnt[o][:, 0:NB], ones[:, 0:1], start=True, stop=True).then_inc(s_p, 1)
                    pe.wait_ge(s_v, 13)
                    nc.tensor.matmul(ps[3][0:NB, 0:1], upto[0:NB, 0:NB], endc[:, 0:1], start=True, stop=True).then_inc(s_p, 1)
                    pe.wait_ge(s_v, 15)
                    nc.tensor.matmul(ps[4][0:1, 0:T], ones[0:NB, 0:1], slot_tmp[0][0:NB, :], start=True,
                                     stop=True).then_inc(s_p, 1)

            s_o2, s_td, s_tc = sem(f"{o}_rank_onehots"), sem(f"{o}_transposed"), sem(f"{o}_transposed_copied")
            s_sd, s_su, s_gd, s_ps = (sem(f"{o}_same_done"), sem(f"{o}_same_masked"), sem(f"{o}_rank_done"),
                                      sem(f"{o}_slots_written"))
            s_rc = sem(f"{o}_rank_chain")
            with nc.Block() as block:
                @block.vector
                def _(v):
                    ch = Chain(v, s_rc)

                    def body(i):
                        ch.start(i)
                        for h in range(2):
                            t0 = i * (2 * G) + h * G
                            wait(v, s_gd, i * 2 + (h - 1))
                            nc.vector.tensor_tensor(oh16[h][:, :, :], iota0[:, None, :].to_broadcast([P, G, P]),
                                                    key["lo"][:, bass.ds(t0, G)].to_broadcast([P, G, P]), ALU.is_equal)
                            nc.vector.tensor_tensor(hi16[h][:, :, :], iota0[:, None, 0:NH].to_broadcast([P, G, NH]),
                                                    key["hi"][:, bass.ds(t0, G)].to_broadcast([P, G, NH]),
                                                    ALU.is_equal).then_inc(s_o2, 1)
                        for h in range(2):
                            v.wait_ge(s_sd, i * 2 + (h + 1))
                            nc.vector.tensor_tensor(same[h][:, :, :], ps[2 + h][:, :].rearrange("p (g n) -> p g n", g=G),
                                                    after[:, None, :].to_broadcast([P, G, P]), ALU.mult).then_inc(s_su, 1)
                        for h in range(2):
                            v.wait_ge(s_gd, i * 2 + (h + 1))
                            pr = prod[h][:, :, 0:NH]
                            ch.link(nc.vector.tensor_tensor(pr, ps[4 + h][:, 0:G * NH].rearrange("p (g n) -> p g n", g=G),
                                                            hi16[h][:, :, :], ALU.mult))
                            nc.vector.tensor_reduce(out=pos[:, bass.ds(i * (2 * G) + h * G, G)], in_=pr, axis=AX_X,
                                                    op=ALU.add).then_inc(s_ps, 1)
                    loop(v, ET // (2 * G), body)

                @block.scalar
                def _(act):
                    def body(i):
                        for h in range(2):
                            act.wait_ge(s_td, i * 2 + (h + 1))
                            wait(act, s_gd, i * 2 + (h - 1))
                            nc.scalar.copy(ohT[h][:, :, :], ps[h][:, :].bitcast(BF16)[:, 0:G * P]
                                           .rearrange("p (g n) -> p g n", g=G)).then_inc(s_tc, 1)
                    loop(act, ET // (2 * G), body)

                @block.tensor
                def _(pe):
                    def body(i):
                        for h in range(2):
                            pe.wait_ge(s_o2, i * 2 + (h + 1))
                            for j in range(G):
                                last = nc.tensor.transpose(ps[h][:, :].bitcast(BF16)[:, j * P:(j + 1) * P],
                                                           oh16[h][:, j, :], ident16[:, :])
                            last.then_inc(s_td, 1)
                        for h in range(2):
                            pe.wait_ge(s_tc, i * 2 + (h + 1))
                            for j in range(G):
                                last = nc.tensor.matmul(ps[2 + h][:, j * P:(j + 1) * P], ohT[h][:, j, :], ohT[h][:, j, :],
                                                        start=True, stop=True)
                            last.then_inc(s_sd, 1)
                        for h in range(2):
                            pe.wait_ge(s_su, i * 2 + (h + 1))
                            wait(pe, s_ps, i * 2 + (h - 1))
                            for j in range(G):
                                to = ps[4 + h][:, j * NH:(j + 1) * NH]
                                nc.tensor.matmul(to, ohT[h][:, j, :], table[:, :, bass.ds(i * (2 * G) + (h * G + j), 1)]
                                                 .rearrange("p h t -> p (h t)"), start=True, stop=False)
                                last = nc.tensor.matmul(to, same[h][:, j, :], hi16[h][:, j, :], start=False, stop=True)
                            last.then_inc(s_gd, 1)
                    loop(pe, ET // (2 * G), body)

            s_pc, s_in, s_pd = sem(f"{o}_slot_chain"), sem(f"{o}_scatter_ready"), sem(f"{o}_scatter_done")
            plo, phi = key["lo"], key["hi"]
            with nc.Block() as block:
                @block.vector
                def _(v):
                    ch = Chain(v, s_pc)
                    ch.link(nc.vector.tensor_copy(keyi[:, :], pos[:, :]))
                    ch.link(nc.vector.tensor_scalar(keyt[:, :], keyi[:, :], 7, None, ALU.arith_shift_right))
                    ch.link(nc.vector.tensor_copy(phi[:, :], keyt[:, :]))
                    ch.link(nc.vector.tensor_scalar(keyt[:, :], keyi[:, :], P - 1, None, ALU.bitwise_and))
                    ch.link(nc.vector.tensor_copy(plo[:, :], keyt[:, :]))

                    def body(i):
                        for h in range(2):
                            wait(v, s_pd, i * 2 + (h - 1))
                            for j in range(G):
                                t = bass.ds(i * (2 * G) + (h * G + j), 1)
                                nc.vector.tensor_scalar(oh16[h][:, j, :], iota0h[:, :], plo[:, t], num_hi[:, t],
                                                        ALU.is_equal, ALU.mult)
                                nc.vector.tensor_scalar(same[h][:, j, :], iota0h[:, :], plo[:, t], num_lo[:, t],
                                                        ALU.is_equal, ALU.mult)
                                last = nc.vector.tensor_scalar(big16[h][:, j, :], iotaTh[:, :], phi[:, t], None, ALU.is_equal)
                            last.then_inc(s_in, 1)
                    loop(v, ET // (2 * G), body)
                    v.wait_ge(s_pd, ET // G)
                    num = slot_tmp[0][:, :]
                    ch.link(nc.vector.tensor_copy(num, ps[7][:, 0:T]))
                    ch.link(nc.vector.scalar_tensor_tensor(out=num, in0=ps[6][:, 0:T], scalar=256.0, in1=num,
                                                           op0=ALU.mult, op1=ALU.add))
                    nc.vector.tensor_scalar(valid[o][:, :], num, 1.0, None, ALU.is_ge)
                    ch.link(nc.vector.tensor_scalar(eidx[o][:, :], num, -1.0, 0.0, ALU.add, ALU.max))

                @block.tensor
                def _(pe):
                    def body(i):
                        for h in range(2):
                            pe.wait_ge(s_in, i * 2 + (h + 1))
                            for j in range(G):
                                first = isinstance(i, int) and i == 0 and h == 0 and j == 0
                                final = isinstance(i, int) and i > 0 and h == 1 and j == G - 1
                                nc.tensor.matmul(ps[6][:, 0:T], oh16[h][:, j, :], big16[h][:, j, :], start=first, stop=final)
                                last = nc.tensor.matmul(ps[7][:, 0:T], same[h][:, j, :], big16[h][:, j, :], start=first,
                                                        stop=final)
                            last.then_inc(s_pd, 1)
                    loop(pe, ET // (2 * G), body, last_too=True)

        def gather(to, table_ap, index, slot):
            nc.gpsimd.indirect_dma_start(to, None, table_ap, bass.IndirectOffsetOnAxis(ap=index, axis=0)) \
              .then_inc(landed[slot], 16)

        def wait_landed(eng, h, value, alone=None):
            for j in range(G):
                if alone is not None:
                    hold(eng, landed[h * G + j], value, alone)
                else:
                    eng.wait_ge(landed[h * G + j], value)

        def block_ids(engines, o, t0):
            _, vals = nc.values_load_multi_w_load_instructions(
                bid[o][0:1, bass.ds(t0, G)], engines=engines, min_val=0, max_val=NB - 1,
                skip_runtime_bounds_check_because="clamped to the last block when it was made")
            return vals

        STEPS = T // (2 * G)

        def edge_rows(o):
            full = o == "dst"
            own_col, other_col = (C_DST, C_SRC) if full else (C_SRC, C_DST)
            s_st, s_used, s_as = sem(f"{o}_staged"), sem(f"{o}_rows_used"), [sem(f"{o}_attr_stored{h}") for h in range(2)]
            s_ch = sem(f"{o}_rows_chain")
            s_oh, s_pt, s_at, s_pq, s_ab = (sem(f"{o}_rows_onehots"), sem(f"{o}_rows_transposed"), sem(f"{o}_rows_copied"),
                                            sem(f"{o}_rows_products"), sem(f"{o}_bias_done"))
            s_vs = [sem(f"{o}_v_stored{h}") for h in range(2)]
            s_ef = sem(f"{o}_features_packed")
            base = 16 * rounds[0]
            per = 2 if full else 1
            with nc.Block() as block:
                @block.gpsimd
                def _(g):
                    def kv(i, h, n_landed):
                        wait_landed(g, h, n_landed, passed["pool"])
                        for j in range(G):
                            gather(grow[h][:, j, :], kv_table, erow[h][:, j, C_SRC:C_SRC + 1].bitcast(I32), h * G + j)

                    def body(i):
                        for h in range(2):
                            hold(g, s_used, i * 2 + (h - 1), passed["pool"])
                            hold(g, s_as[h], i * 16, passed["pool"])
                            if full:
                                hold(g, s_vs[h], i * 16, passed["pool"])
                            nc.gpsimd.tensor_copy(stage[h][:, :], eidx[o][:, bass.ds(i * (2 * G) + h * G, G)]).then_inc(s_st, 1)
                            hold(g, s_st, i * 2 + (h + 1), passed["pool"])
                            for j in range(G):
                                gather(erow[h][:, j, :], edge_table, stage[h][:, j:j + 1], h * G + j)
                        if full:
                            for h in range(2):
                                kv(i, h, i * 32 + (base + 16))
                    loop(g, STEPS, body)

                @block.sync
                def _(sp):
                    def body(i):
                        for h in range(2):
                            t = bass.ds(i * (2 * G) + h * G, G)
                            wait_landed(sp, h, i * (16 * per) + (base + 16))
                            sp.dma_start(a_rows[o][t, :, :].rearrange("t p c -> p t c"),
                                         erow[h][:, :, 0:FE64]).then_inc(s_as[h], 16)
                        if full:
                            for h in range(2):
                                t = bass.ds(i * (2 * G) + h * G, G)
                                wait_landed(sp, h, i * (16 * per) + (base + 32))
                                sp.dma_start(v_rows[t, :, :].rearrange("t p c -> p t c"),
                                             grow[h][:, :, D:2 * D]).then_inc(s_vs[h], 16)
                    loop(sp, STEPS, body)
                    for h in range(2):
                        sp.wait_ge(s_as[h], 16 * STEPS)
                        if full:
                            sp.wait_ge(s_vs[h], 16 * STEPS)

                @block.vector
                def _(v):
                    ch = Chain(v, s_ch)

                    def body(i):
                        ch.start(i)
                        for h in range(2):
                            t = bass.ds(i * (2 * G) + h * G, G)
                            wait_landed(v, h, i * (16 * per) + (base + 16))
                            rows = erow[h]
                            own = rows[:, :, own_col:own_col + 1].bitcast(I32).rearrange("p g o -> p (g o)")
                            oth = rows[:, :, other_col:other_col + 1].bitcast(I32).rearrange("p g o -> p (g o)")
                            ch.link(nc.vector.tensor_scalar(tinyi[h][:, :], own, P - 1, None, ALU.bitwise_and))
                            nc.vector.tensor_scalar(other[o][:, t], oth, 0.0, None, ALU.add)
                            ch.link(nc.vector.scalar_tensor_tensor(out=lo1[o][:, t], in0=tinyi[h][:, :], scalar=1.0,
                                                                   in1=valid[o][:, t], op0=ALU.add, op1=ALU.mult))
                            nc.vector.scalar_tensor_tensor(out=node[o][:, t], in0=own, scalar=1.0, in1=valid[o][:, t],
                                                           op0=ALU.add, op1=ALU.mult)
                            if full:
                                nc.vector.tensor_tensor(oh16[h][:, :, :], iota1[:, None, :].to_broadcast([P, G, P]),
                                                        lo1[o][:, t].to_broadcast([P, G, P]), ALU.is_equal).then_inc(s_oh, 1)
                            ch.link(nc.vector.tensor_tensor(prod[h][:, :, 0:FE64], rows[:, :, 0:FE64],
                                                            wge[:, None, :].to_broadcast([P, G, FE64]), ALU.mult))
                            last = nc.vector.tensor_reduce(out=ge[o][:, t], in_=prod[h][:, :, 0:FE64], axis=AX_X, op=ALU.add)
                            if full:
                                ch.link(last)
                            else:
                                last.then_inc(s_used, 1)
                        if full:
                            for h in range(2):
                                t = bass.ds(i * (2 * G) + h * G, G)
                                wait_landed(v, h, i * 32 + (base + 32))
                                v.wait_ge(s_pq, i * 2 + (h + 1))
                                ch.link(nc.vector.tensor_tensor(prod[h][:, :, :],
                                                                ps[4 + h][:, :].rearrange("p (g n) -> p g n", g=G),
                                                                grow[h][:, :, 0:D], ALU.mult))
                                qk = tiny[h][:, 0, :]
                                ch.link(nc.vector.tensor_reduce(out=qk, in_=prod[h][:, :, :].rearrange("p g (h c) -> p (g h) c", c=C),
                                                                axis=AX_X, op=ALU.add))
                                nvc = grow[h][:, :, 2 * D:KVW].rearrange("p g o -> p (g o)")
                                nc.vector.tensor_scalar(S[:, t, H:H + 1].rearrange("p g o -> p (g o)"), nvc, 1.0, None, ALU.mult)
                                nc.vector.scalar_tensor_tensor(
                                    out=S[:, t, 0:H], in0=qk.rearrange("p (g h) -> p g h", h=H), scalar=1.0 / C ** 0.5,
                                    in1=ps[2 + h][:, P:P + G * H].rearrange("p (g h) -> p g h", h=H),
                                    op0=ALU.mult, op1=ALU.add).then_inc(s_used, 1)
                    loop(v, STEPS, body)

                if full:
                    @block.scalar
                    def _(act):
                        def body(i):
                            for h in range(2):
                                wait_landed(act, h, i * 32 + (base + 16))
                                wait(act, s_pq, i * 2 + (h - 1))
                                nc.scalar.copy(efeat[h][:, :].rearrange("p (g f) -> p g f", g=G),
                                               erow[h][:, :, FE64:FE64 + FE32]).then_inc(s_ef, 1)
                                act.wait_ge(s_pt, i * 4 + (2 * h + 1))
                                nc.scalar.copy(xt[:, h, :], ps[2 + h][:, 0:P]).then_inc(s_at, 1)
                                act.wait_ge(s_pt, i * 4 + (2 * h + 2))
                                nc.scalar.copy(ohT[h][:, :, :], ps[h][:, :].bitcast(BF16)[:, 0:G * P]
                                               .rearrange("p (g n) -> p g n", g=G)).then_inc(s_at, 1)
                        loop(act, STEPS, body)

                    @block.tensor
                    def _(pe):
                        def body(i):
                            for h in range(2):
                                blocks = block_ids(PE_ONLY, o, i * (2 * G) + h * G)
                                pe.wait_ge(s_ef, i * 2 + (h + 1))
                                wait(pe, s_used, i * 2 + (h - 1))
                                nc.tensor.transpose(ps[2 + h][:, 0:P], efeat[h][:, :], ident[:, :]).then_inc(s_pt, 1)
                                pe.wait_ge(s_oh, i * 2 + (h + 1))
                                for j in range(G):
                                    last = nc.tensor.transpose(ps[h][:, :].bitcast(BF16)[:, j * P:(j + 1) * P],
                                                               oh16[h][:, j, :], ident16[:, :])
                                last.then_inc(s_pt, 1)
                                pe.wait_ge(s_at, i * 4 + (2 * h + 2))
                                nc.tensor.matmul(ps[2 + h][:, P:P + G * H], xt[:, h, :], we_bd[:, :], start=True, stop=True)
                                for j in range(G):
                                    last = nc.tensor.matmul(ps[4 + h][:, j * P:(j + 1) * P], ohT[h][:, j, :],
                                                            qs[:, bass.ds(blocks[j], 1), :].rearrange("p o d -> p (o d)"),
                                                            start=True, stop=True)
                                last.then_inc(s_pq, 1)
                        loop(pe, STEPS, body)
            rounds[0] += per * STEPS

        def segment_max(name, o, channels, flags):
            s_v, s_p, s_a = sem(f"{name}_scan"), sem(f"{name}_scan_pe"), sem(f"{name}_scan_act")
            keys_s, keep_f, keep_b, val, res, tmp = scan
            thr_f, thr_b = colsA[0:SR, 0, 0:1], colsA[0:SR, 0, 1:2]
            cnt_v, cnt_p = [0], [0]

            plan = []
            with nc.Block() as block:
                def turn(build_pe, build_dve):
                    plan.append((build_pe, build_dve))

                def to_scan(src, dst):
                    def pe_part():
                        for k in range(4):
                            last = nc.tensor.transpose(ps[k][0:SR, 0:P], src[:, k:T:4], ident[:, :])
                        return last

                    def dve_part(link):
                        for k in range(4):
                            ins = nc.vector.tensor_copy(dst[:, k * P:(k + 1) * P], ps[k][0:SR, 0:P])
                        link(ins)
                    turn(pe_part, dve_part)

                def to_slots(src, dst):
                    def pe_part():
                        for k in range(4):
                            last = nc.tensor.transpose(ps[k][:, 0:SR], src[:, k * P:(k + 1) * P], ident[0:SR, 0:SR])
                        return last

                    def dve_part(link):
                        for k in range(4):
                            ins = nc.vector.tensor_copy(dst[:, k:T:4], ps[k][:, 0:SR])
                        link(ins)
                    turn(pe_part, dve_part)

                to_scan(node[o][:, :], keys_s)

                def edge_keys():
                    nc.tensor.matmul(ps[4][0:SR, 0:1], down1[0:SR, 0:SR], keys_s[:, SL - 1:SL], start=True, stop=True)
                    return nc.tensor.matmul(ps[4][0:SR, 1:2], up1[0:SR, 0:SR], keys_s[:, 0:1], start=True, stop=True)

                def edge_flags(link):
                    nc.vector.tensor_tensor(keep_f[:, 1:SL], keys_s[:, 1:SL], keys_s[:, 0:SL - 1], ALU.is_equal)
                    nc.vector.tensor_tensor(keep_f[:, 0:1], keys_s[:, 0:1], ps[4][0:SR, 0:1], ALU.is_equal)
                    nc.vector.tensor_tensor(keep_b[:, 0:SL - 1], keys_s[:, 0:SL - 1], keys_s[:, 1:SL], ALU.is_equal)
                    link(nc.vector.tensor_tensor(keep_b[:, SL - 1:SL], keys_s[:, SL - 1:SL], ps[4][0:SR, 1:2], ALU.is_equal))
                    if flags:
                        link(nc.vector.tensor_scalar(val, keep_b, -1.0, 1.0, ALU.mult, ALU.add))
                    link(nc.vector.tensor_reduce(out=thr_f, in_=keep_f, axis=AX_X, op=ALU.min))
                    link(nc.vector.tensor_reduce(out=thr_b, in_=keep_b, axis=AX_X, op=ALU.min))
                    for f in (keep_f, keep_b, colsA[0:SR, 0, 0:2]):
                        link(nc.vector.tensor_scalar(f, f, 2 * 1.5e38, -1.5e38, ALU.mult, ALU.add))
                turn(edge_keys, edge_flags)
                if flags:
                    to_slots(val, is_last[o])
                for values, maxima in channels:
                    to_scan(values, val)
                    for back in (False, True):
                        keep = keep_b if back else keep_f
                        a, r = (res, tmp) if back else (val, res)
                        edge = 0 if back else SL - 1
                        shift = up1 if back else down1

                        def rev(ap, back=back):
                            return ap[:, ::-1] if back else ap

                        def open_scan(link, a=a, r=r, keep=keep, edge=edge, rev=rev, back=back):
                            link(nc.vector.tensor_tensor_scan(rev(r), rev(keep), rev(a), -BIG, ALU.min, ALU.max))
                            link(nc.vector.tensor_copy(colsA[0:SR, 1, 0:1], r[:, edge:edge + 1]))
                            link(nc.vector.tensor_copy(colsA[0:SR, 1, 1:2], (thr_b if back else thr_f)))
                        plan[-1] = (plan[-1][0], lambda link, old=plan[-1][1], new=open_scan: (old(link), new(link)))

                        def rows_up():
                            nc.tensor.transpose(ps[5][0:1, 0:SR], colsA[0:SR, 1, 0:1], ident[0:SR, 0:SR])
                            return nc.tensor.transpose(ps[6][0:1, 0:SR], colsA[0:SR, 1, 1:2], ident[0:SR, 0:SR])

                        def row_scan(link, rev=rev):
                            nc.vector.tensor_copy(rowsA[0:1, 0, 0:SR], ps[5][0:1, 0:SR])
                            link(nc.vector.tensor_copy(rowsA[0:1, 1, 0:SR], ps[6][0:1, 0:SR]))
                            link(nc.vector.tensor_tensor_scan(rev(rowsA[0:1, 2, 0:SR]), rev(rowsA[0:1, 1, 0:SR]),
                                                              rev(rowsA[0:1, 0, 0:SR]), -BIG, ALU.min, ALU.max))
                            link(nc.vector.memset(rowsA[0:1, 3, 0:SR], -1.5e38))
                            if rev(ident) is ident:
                                link(nc.vector.tensor_copy(rowsA[0:1, 3, 1:SR], rowsA[0:1, 2, 0:SR - 1]))
                            else:
                                link(nc.vector.tensor_copy(rowsA[0:1, 3, 0:SR - 1], rowsA[0:1, 2, 1:SR]))
                        turn(rows_up, row_scan)

                        def rows_down():
                            return nc.tensor.transpose(ps[7][0:SR, 0:1], rowsA[0:1, 3, 0:SR], ident[0:1, 0:1])

                        def final_scan(link, a=a, r=r, keep=keep, rev=rev):
                            link(nc.vector.tensor_copy(colsA[0:SR, 2, 0:1], ps[7][0:SR, 0:1]))
                            link(nc.vector.tensor_tensor_scan(rev(r), rev(keep), rev(a), colsA[0:SR, 2, 0:1],
                                                              ALU.min, ALU.max))
                        turn(rows_down, final_scan)
                    to_slots(tmp, maxima)

                marks = []

                @block.vector
                def _(v):
                    ch = Chain(v, s_v)
                    for n, (_, dve_part) in enumerate(plan):
                        v.wait_ge(s_p, n + 1)
                        dve_part(ch.link)
                        marks.append(ch.k)

                @block.tensor
                def _(pe):
                    for n, (pe_part, _) in enumerate(plan):
                        if n:
                            pe.wait_ge(s_v, marks[n - 1])
                        pe_part().then_inc(s_p, 1)

        def aggregate(name, o, cols, build, loads=(), table_ap=None, index=None, width=0):
            view = acc[:, 0:NB * cols].rearrange("p (b c) -> p b c", b=NB)
            s_st, s_z = sem(f"{name}_staged"), sem(f"{name}_chain")
            s_in, s_rd, s_pd, s_ad = ([sem(f"{name}_loaded{h}") for h in range(2)], sem(f"{name}_rhs_ready"),
                                      sem(f"{name}_summed"), sem(f"{name}_added"))
            base = 16 * rounds[0]
            with nc.Block() as block:
                if loads:
                    @block.sync
                    def _(sp):
                        def body(i):
                            for h in range(2):
                                wait(sp, s_rd, i * 2 + (h - 1))
                                for buf, rows in loads:
                                    sp.dma_start(buf[h], rows[bass.ds(i * (2 * G) + h * G, G), :, :]
                                                 .rearrange("t p c -> p t c")).then_inc(s_in[h], 16)
                        loop(sp, STEPS, body)

                if table_ap is not None:
                    @block.gpsimd
                    def _(g):
                        def body(i):
                            for h in range(2):
                                hold(g, s_pd, i * 2 + (h - 1), passed["pool"])
                                nc.gpsimd.tensor_copy(stage[h][:, :], index[:, bass.ds(i * (2 * G) + h * G, G)]).then_inc(s_st, 1)
                                hold(g, s_st, i * 2 + (h + 1), passed["pool"])
                                for j in range(G):
                                    gather(grow[h][:, j, 0:width], table_ap, stage[h][:, j:j + 1], h * G + j)
                        loop(g, STEPS, body)

                @block.vector
                def _(v):
                    ch = Chain(v, s_z)
                    nc.vector.memset(acc[:, 0:NB * cols], 0.0)

                    def add(i, h):
                        blocks = block_ids(DVE_ONLY, o, i * (2 * G) + h * G)
                        v.wait_ge(s_pd, i * 2 + (h + 1))
                        for j in range(G):
                            at = view[:, bass.ds(blocks[j], 1), :].rearrange("p o c -> p (o c)")
                            nc.vector.tensor_tensor(at, at, ps[h * G + j][:, 0:cols], ALU.add).then_inc(s_ad, 1)
                            v.wait_ge(s_ad, i * (2 * G) + (h * G + j + 1))

                    def body(i):
                        ch.start(i)
                        for h in range(2):
                            t = bass.ds(i * (2 * G) + h * G, G)
                            wait(v, s_pd, i * 2 + (h - 1))
                            nc.vector.tensor_tensor(oh[h][:, :, :], iota1[:, None, :].to_broadcast([P, G, P]),
                                                    lo1[o][:, t].to_broadcast([P, G, P]), ALU.is_equal)
                            if loads:
                                v.wait_ge(s_in[h], i * (16 * len(loads)) + 16 * len(loads))
                            if table_ap is not None:
                                wait_landed(v, h, i * 16 + (base + 16))
                            build(ch.link, t, h).then_inc(s_rd, 1)
                        for h in range(2):
                            add(i, h)
                    loop(v, STEPS, body)

                @block.tensor
                def _(pe):
                    def body(i):
                        for h in range(2):
                            pe.wait_ge(s_rd, i * 2 + (h + 1))
                            wait(pe, s_ad, i * (2 * G) + (h * G - G))
                            for j in range(G):
                                last = nc.tensor.matmul(ps[h * G + j][:, 0:cols], oh[h][:, j, :], rhs[h][:, j, 0:cols],
                                                        start=True, stop=True)
                            last.then_inc(s_pd, 1)
                    loop(pe, STEPS, body)
            if table_ap is not None:
                rounds[0] += STEPS
            return view

        def look_up(name, o, write, table_ap=None, index=None, width=0, keep_rows=None, extra=None):
            s_st, s_oh, s_td, s_tc, s_pd, s_wr = (sem(f"{name}_{k}") for k in
                                                  ("staged", "onehots", "transposed", "copied", "looked_up", "written"))
            s_hs = [sem(f"{name}_stored{h}") for h in range(2)]
            base = 16 * rounds[0]
            with nc.Block() as block:
                if table_ap is not None:
                    @block.gpsimd
                    def _(g):
                        def body(i):
                            for h in range(2):
                                hold(g, s_wr, i * 2 + (h - 1), passed["pool"])
                                hold(g, s_hs[h], i * 16, passed["pool"])
                                nc.gpsimd.tensor_copy(stage[h][:, :], index[:, bass.ds(i * (2 * G) + h * G, G)]).then_inc(s_st, 1)
                                hold(g, s_st, i * 2 + (h + 1), passed["pool"])
                                for j in range(G):
                                    gather(grow[h][:, j, 0:width], table_ap, stage[h][:, j:j + 1], h * G + j)
                        loop(g, STEPS, body)

                    @block.sync
                    def _(sp):
                        def body(i):
                            for h in range(2):
                                wait_landed(sp, h, i * 16 + (base + 16))
                                sp.dma_start(keep_rows[bass.ds(i * (2 * G) + h * G, G), :, :].rearrange("t p c -> p t c"),
                                             grow[h][:, :, 0:FE64]).then_inc(s_hs[h], 16)
                        loop(sp, STEPS, body)
                        for h in range(2):
                            sp.wait_ge(s_hs[h], 16 * STEPS)

                @block.vector
                def _(v):
                    def body(i):
                        for h in range(2):
                            t = bass.ds(i * (2 * G) + h * G, G)
                            wait(v, s_td, i * 2 + (h - 1))
                            nc.vector.tensor_tensor(oh16[h][:, :, :], iota1[:, None, :].to_broadcast([P, G, P]),
                                                    lo1[o][:, t].to_broadcast([P, G, P]), ALU.is_equal).then_inc(s_oh, 1)
                        for h in range(2):
                            t = bass.ds(i * (2 * G) + h * G, G)
                            if table_ap is not None:
                                wait_landed(v, h, i * 16 + (base + 16))
                                extra(t, h)
                            v.wait_ge(s_pd, i * 2 + (h + 1))
                            write(t, ps[4 + h][:, 0:4 * G].rearrange("p (g k) -> p g k", g=G)).then_inc(s_wr, 1)
                    loop(v, STEPS, body)

                @block.scalar
                def _(act):
                    def body(i):
                        for h in range(2):
                            act.wait_ge(s_td, i * 2 + (h + 1))
                            wait(act, s_pd, i * 2 + (h - 1))
                            nc.scalar.copy(ohT[h][:, :, :], ps[h][:, :].bitcast(BF16)[:, 0:G * P]
                                           .rearrange("p (g n) -> p g n", g=G)).then_inc(s_tc, 1)
                    loop(act, STEPS, body)

                @block.tensor
                def _(pe):
                    def body(i):
                        for h in range(2):
                            pe.wait_ge(s_oh, i * 2 + (h + 1))
                            wait(pe, s_tc, i * 2 + (h - 1))
                            for j in range(G):
                                last = nc.tensor.transpose(ps[h][:, :].bitcast(BF16)[:, j * P:(j + 1) * P],
                                                           oh16[h][:, j, :], ident16[:, :])
                            last.then_inc(s_td, 1)
                        for h in range(2):
                            blocks = block_ids(PE_ONLY, o, i * (2 * G) + h * G)
                            pe.wait_ge(s_tc, i * 2 + (h + 1))
                            wait(pe, s_wr, i * 2 + (h - 1))
                            for j in range(G):
                                last = nc.tensor.matmul(ps[4 + h][:, 4 * j:4 * j + 4], ohT[h][:, j, :],
                                                        node_vals[:, bass.ds(blocks[j], 1), :].rearrange("p o d -> p (o d)"),
                                                        start=True, stop=True)
                            last.then_inc(s_pd, 1)
                    loop(pe, STEPS, body)
            if table_ap is not None:
                rounds[0] += STEPS

        def node_products(name, source, width, weights, take, store=None, before=None, groups=None):
            s_b, s_t, s_c, s_p, s_k = (sem(f"{name}_{k}") for k in ("input", "transposed", "copied", "product", "taken"))
            s_s = [sem(f"{name}_stored{k}") for k in range(2)]
            with nc.Block() as block:
                @block.vector
                def _(v):
                    if before is not None:
                        before(Chain(v, s_b))
                    for b in range(NB):
                        v.wait_ge(s_p, b + 1)
                        if store is not None and b >= 2:
                            v.wait_ge(s_s[b % 2], 16 * (b // 2))
                        take(b, ps[4 + b % 4][:, 0:width]).then_inc(s_k, 1)

                @block.tensor
                def _(pe):
                    if before is not None:
                        pe.wait_ge(s_b, before.links)
                    for b in range(NB + 1):
                        if b < NB:
                            k = source(b).shape[-1]
                            if b >= 4:
                                pe.wait_ge(s_c, b - 3)
                            nc.tensor.transpose(ps[b % 4][0:k, 0:P], source(b), ident[:, :]).then_inc(s_t, 1)
                        if b:
                            pe.wait_ge(s_c, b)
                            if b > 4:
                                pe.wait_ge(s_k, b - 4)
                            nc.tensor.matmul(ps[4 + (b - 1) % 4][:, 0:width], xt[0:weights.shape[0], (b - 1) % 4, :], weights,
                                             start=True, stop=True).then_inc(s_p, 1)

                @block.scalar
                def _(act):
                    for b in range(NB):
                        k = source(b).shape[-1]
                        act.wait_ge(s_t, b + 1)
                        if b >= 4:
                            act.wait_ge(s_p, b - 3)
                        nc.scalar.copy(xt[0:k, b % 4, :], ps[b % 4][0:k, 0:P]).then_inc(s_c, 1)

                if store is not None:
                    @block.sync
                    def _(sp):
                        for b in range(NB):
                            sp.wait_ge(s_k, b + 1)
                            sp.dma_start(store[b * P:(b + 1) * P, :], nout[:, b % 2, 0:width if store is not kv_table else KVW]) \
                              .then_inc(s_s[b % 2], 16)
                        for k in range(2):
                            sp.wait_ge(s_s[k], 16 * ((NB + 1 - k) // 2))

        def bc(ap, shape):
            return ap.to_broadcast(shape)

        def layer_norm(name, update):
            s_v, s_r = sem(f"{name}_norm"), sem(f"{name}_root")
            marks = []
            with nc.Block() as block:
                @block.vector
                def _(v):
                    ch = Chain(v, s_v)
                    update(ch.link)
                    mean, var = small[:, 6, 0:NB], small[:, 7, 0:NB]
                    ch.link(nc.vector.tensor_tensor(xs[:, :, :], xs[:, :, :], wide, ALU.add))
                    ch.link(nc.vector.tensor_reduce(out=mean, in_=xs[:, :, :], axis=AX_X, op=ALU.add))
                    ch.link(nc.vector.tensor_scalar(mean, mean, 1.0 / D, None, ALU.mult))
                    ch.link(nc.vector.tensor_tensor(xs[:, :, :], xs[:, :, :], bc(mean, [P, NB, D]), ALU.subtract))
                    ch.link(nc.vector.tensor_tensor(wide, xs[:, :, :], xs[:, :, :], ALU.mult))
                    ch.link(nc.vector.tensor_reduce(out=var, in_=wide, axis=AX_X, op=ALU.add))
                    ch.link(nc.vector.tensor_scalar(var, var, 1.0 / D, EPS, ALU.mult, ALU.add))
                    marks.append(ch.k)
                    v.wait_ge(s_r, 1)
                    ch.link(nc.vector.reciprocal(var, var))
                    ch.link(nc.vector.tensor_tensor(xs[:, :, :], xs[:, :, :], bc(var, [P, NB, D]), ALU.mult))

                @block.scalar
                def _(act):
                    act.wait_ge(s_v, marks[0])
                    nc.scalar.activation(small[:, 7, 0:NB], small[:, 7, 0:NB], ACT.Sqrt).then_inc(s_r, 1)

        def take_qkv(b, product):
            nc.vector.tensor_copy(qs[:, b, :], product[:, 0:D])
            nc.vector.tensor_copy(nout[:, b % 2, 2 * D:KVW], nv[:, b:b + 1])
            return nc.vector.tensor_copy(nout[:, b % 2, 0:2 * D], product[:, D:3 * D])

        node_products("qkv", lambda b: xs[:, b, :], 3 * D, wqkv[:, :], take_qkv, store=kv_table)
        s_tw = sem("table_wait")
        with nc.Block() as block:
            @block.gpsimd
            def _(g):
                g.wait_ge(s_t, 32)
        recycle()
        sort("dst", 0)
        recycle()
        sort("src", 1)
        recycle()
        edge_rows("dst")

        s_l3 = sem("l3_logits")
        with nc.Block() as block:
            @block.vector
            def _(v):
                ch = Chain(v, s_l3)
                e = slot_tmp[3][:, :]
                ch.link(nc.vector.tensor_copy(e, S[:, :, H]))
                ch.link(nc.vector.scalar_tensor_tensor(out=S[:, :, H], in0=e, scalar=0.2, in1=e, op0=ALU.mult, op1=ALU.max))
                ch.link(nc.vector.tensor_scalar(slot_tmp[2][:, :], e, -1.0, None, ALU.mult))
                ch.link(nc.vector.scalar_tensor_tensor(out=S[:, :, H + 1], in0=slot_tmp[2][:, :], scalar=0.2,
                                                       in1=slot_tmp[2][:, :], op0=ALU.mult, op1=ALU.max))
        e3 = slot_tmp[3]
        M = work[:, 6 * SL:6 * SL + T * KD].rearrange("p (t c) -> p t c", c=KD)
        segment_max("dst", "dst", [(S[:, :, c], M[:, :, c]) for c in range(KD)] + [(ge["dst"][:, :], gm_slot[:, :])], True)
        s_x0, s_x1 = sem("exp_arguments"), sem("exp_done")
        l3w = [sb(f"l3w{k}", [P, T]) for k in range(2)]
        with nc.Block() as block:
            @block.vector
            def _(v):
                nc.vector.tensor_tensor(S[:, :, :], S[:, :, :], M[:, :, :], ALU.subtract).then_inc(s_x0, 1)

            @block.scalar
            def _(act):
                act.wait_ge(s_x0, 1)
                nc.scalar.activation(S[:, :, :], S[:, :, :], ACT.Exp).then_inc(s_x1, 1)

            @block.gpsimd
            def _(g):
                g.wait_ge(s_x1, 1)
                nc.gpsimd.tensor_copy(l3w[0][:, :], S[:, :, H])
                nc.gpsimd.tensor_copy(l3w[1][:, :], S[:, :, H + 1])

        def build0(link, t, h):
            ex = S[:, t, 0:H]
            nc.vector.tensor_tensor(rhs[h][:, :, 0:D].rearrange("p g (h c) -> p g h c", c=C),
                                    grow[h][:, :, 0:D].rearrange("p g (h c) -> p g h c", c=C),
                                    bc(ex, [P, G, H, C]), ALU.mult)
            nc.vector.tensor_scalar(rhs[h][:, :, D:D + H], ex, 1.0, None, ALU.mult)
            return nc.vector.tensor_tensor(rhs[h][:, :, D + H:D + H + 1].rearrange("p g o -> p (g o)"), gm_slot[:, t],
                                           is_last["dst"][:, t], ALU.mult)

        a0 = aggregate("l0", "dst", D + H + 1, build0, loads=[([grow[h][:, :, 0:D] for h in range(2)], v_rows)])

        def update0(link):
            den = prod[0][:, :, :].rearrange("p g n -> p (g n)")[:, 0:NB * H].rearrange("p (b h) -> p b h", b=NB)
            link(nc.vector.tensor_copy(gmax["dst"][:, :], a0[:, :, D + H]))
            link(nc.vector.tensor_scalar(den, a0[:, :, D:D + H], 1e-30, None, ALU.max))
            link(nc.vector.reciprocal(den, den))
            link(nc.vector.tensor_tensor(wide.rearrange("p b (h c) -> p b h c", c=C),
                                         a0[:, :, 0:D].rearrange("p b (h c) -> p b h c", c=C),
                                         bc(den, [P, NB, H, C]), ALU.mult))

        layer_norm("l0", update0)

        recycle()

        dinv = sb("dinv", [P, NB])
        s_d0, s_d1 = sem("degree_ready"), sem("degree_root")
        with nc.Block() as block:
            @block.vector
            def _(v):
                nc.vector.tensor_scalar(dinv[:, :], cnt["src"][:, 0:NB], 1.0, None, ALU.max).then_inc(s_d0, 1)
                v.wait_ge(s_d1, 1)
                nc.vector.reciprocal(dinv[:, :], dinv[:, :]).then_inc(s_d0, 1)
                nc.vector.tensor_scalar(small[:, 0, 0:NB], cnt["src"][:, 0:NB], 0.0, None, ALU.is_gt).then_inc(s_d0, 1)
                v.wait_ge(s_d0, 3)
                nc.vector.tensor_tensor(dinv[:, :], dinv[:, :], small[:, 0, 0:NB], ALU.mult)

            @block.scalar
            def _(act):
                act.wait_ge(s_d0, 1)
                nc.scalar.activation(dinv[:, :], dinv[:, :], ACT.Sqrt).then_inc(s_d1, 1)

        node_products("l1", lambda b: xs[:, b, :], D, w1[:, :],
                      lambda b, product: nc.vector.tensor_scalar(nout[:, b % 2, 0:D], product, dinv[:, b:b + 1], None, ALU.mult),
                      store=y_table)
        edge_rows("src")
        segment_max("src", "src", [(ge["src"][:, :], gm_slot[:, :])], True)

        def build1(link, t, h):
            nc.vector.tensor_scalar(rhs[h][:, :, 0:D], grow[h][:, :, 0:D], 1.0, None, ALU.mult)
            return nc.vector.tensor_tensor(rhs[h][:, :, D:D + 1].rearrange("p g o -> p (g o)"), gm_slot[:, t],
                                           is_last["src"][:, t], ALU.mult)

        a1 = aggregate("l1", "src", D + 1, build1, table_ap=y_table, index=other["src"], width=D)

        def update1(link):
            link(nc.vector.tensor_copy(gmax["src"][:, :], a1[:, :, D]))
            link(nc.vector.tensor_tensor(wide, a1[:, :, 0:D], bc(dinv[:, :], [P, NB, D]), ALU.mult))
            link(nc.vector.tensor_tensor(wide, wide, bc(b1[:, None, :], [P, NB, D]), ALU.add))
            link(nc.vector.tensor_scalar(wide, wide, 0.0, None, ALU.max))

        layer_norm("l1", update1)

        recycle()

        nodes2 = work[:, NB * D:NB * (D + WN)].rearrange("p (b c) -> p b c", b=NB)

        def take2(b, product):
            nc.vector.tensor_copy(nodes2[:, b, :], product)
            return nc.vector.tensor_copy(nout[:, b % 2, 0:WN], product)

        node_products("l2", lambda b: xs[:, b, :], WN, wn[:, :], take2, store=n_table)
        s_n2 = sem("node_values2")
        with nc.Block() as block:
            @block.vector
            def _(v):
                ch = Chain(v, s_n2)
                for k, col in enumerate((65, 64, 66)):
                    ch.link(nc.vector.tensor_copy(node_vals[:, :, k], nodes2[:, :, col]))
                for o in ("dst", "src"):
                    ch.link(nc.vector.tensor_scalar(small[:, 0, 0:NB], cnt[o][:, 0:NB], 0.0, -1e30, ALU.is_equal, ALU.mult))
                    ch.link(nc.vector.tensor_tensor(gmax[o][:, :], gmax[o][:, :], small[:, 0, 0:NB], ALU.add))
                m = small[:, 1, 0:NB]
                ch.link(nc.vector.tensor_tensor(m, gmax["dst"][:, :], gmax["src"][:, :], ALU.max))
                ch.link(nc.vector.tensor_tensor(m, m, node_vals[:, :, 2], ALU.add))
                ch.link(nc.vector.scalar_tensor_tensor(out=node_vals[:, :, 3], in0=m, scalar=0.05, in1=m,
                                                       op0=ALU.mult, op1=ALU.max))

        hj_slot = slot_tmp[0]

        def extra2(t, h):
            nc.vector.tensor_scalar(hj_slot[:, t], grow[h][:, :, 64:65].rearrange("p g o -> p (g o)"), 1.0, None, ALU.mult)

        look_up("l2src", "src", lambda t, product: nc.vector.tensor_scalar(selfv[:, t, :], product, 1.0, None, ALU.mult),
                table_ap=n_table, index=other["src"], width=WN, keep_rows=h_rows, extra=extra2)

        def edge_weights(name, o):
            s_e, s_f = sem(f"{name}_edge_arguments"), sem(f"{name}_edge_exp")
            with nc.Block() as block:
                @block.vector
                def _(v):
                    ch = Chain(v, s_e)
                    w = exe[o][:, :]
                    ch.link(nc.vector.tensor_tensor(w, ge[o][:, :], selfv[:, :, 2], ALU.add))
                    ch.link(nc.vector.scalar_tensor_tensor(out=w, in0=w, scalar=0.05, in1=w, op0=ALU.mult, op1=ALU.max))
                    ch.link(nc.vector.tensor_tensor(w, w, selfv[:, :, 3], ALU.subtract))
                    ch.link(nc.vector.tensor_scalar(w, w, 0.0, None, ALU.min))

                @block.scalar
                def _(act):
                    act.wait_ge(s_e, 4)
                    nc.scalar.activation(exe[o][:, :], exe[o][:, :], ACT.Exp).then_inc(s_f, 1)

        edge_weights("src", "src")
        s_g2 = sem("l2_node_max")
        with nc.Block() as block:
            @block.vector
            def _(v):
                nc.vector.tensor_tensor(slot_tmp[1][:, :], hj_slot[:, :], selfv[:, :, 1], ALU.max)
        segment_max("l2", "src", [(slot_tmp[1][:, :], slot_tmp[2][:, :])], False)
        mslot, exn = slot_tmp[2], slot_tmp[1]
        s_e2, s_f2 = sem("l2_arguments"), sem("l2_exp")
        with nc.Block() as block:
            @block.vector
            def _(v):
                ch = Chain(v, s_e2)
                m, w = mslot[:, :], exn[:, :]
                ch.link(nc.vector.tensor_tensor(m, m, selfv[:, :, 0], ALU.add))
                ch.link(nc.vector.scalar_tensor_tensor(out=m, in0=m, scalar=0.05, in1=m, op0=ALU.mult, op1=ALU.max))
                ch.link(nc.vector.tensor_tensor(w, hj_slot[:, :], selfv[:, :, 0], ALU.add))
                ch.link(nc.vector.scalar_tensor_tensor(out=w, in0=w, scalar=0.05, in1=w, op0=ALU.mult, op1=ALU.max))
                ch.link(nc.vector.tensor_tensor(w, w, m, ALU.subtract))
                ch.link(nc.vector.tensor_scalar(w, w, 0.0, None, ALU.min))
                ch.link(nc.vector.tensor_tensor(m, m, is_last["src"][:, :], ALU.mult))

            @block.scalar
            def _(act):
                act.wait_ge(s_e2, 6)
                nc.scalar.activation(exn[:, :], exn[:, :], ACT.Exp).then_inc(s_f2, 1)

        A = FE64

        def flat(ap):
            return ap.rearrange("p g o -> p (g o)")

        def build2(link, t, h):
            nc.vector.tensor_tensor(rhs[h][:, :, 0:A], grow[h][:, :, 0:A], bc(exn[:, t], [P, G, A]), ALU.mult)
            nc.vector.tensor_tensor(rhs[h][:, :, A:2 * A], arow[h][:, :, :], bc(exe["src"][:, t], [P, G, A]), ALU.mult)
            nc.vector.tensor_scalar(flat(rhs[h][:, :, 2 * A:2 * A + 1]), exn[:, t], 1.0, None, ALU.mult)
            nc.vector.tensor_scalar(flat(rhs[h][:, :, 2 * A + 1:2 * A + 2]), exe["src"][:, t], 1.0, None, ALU.mult)
            return nc.vector.tensor_scalar(flat(rhs[h][:, :, 2 * A + 2:2 * A + 3]), mslot[:, t], 1.0, None, ALU.mult)

        a2 = aggregate("l2s", "src", 2 * A + 3, build2,
                       loads=[([grow[h][:, :, 0:A] for h in range(2)], h_rows),
                              ([arow[h][:, :, :] for h in range(2)], a_rows["src"])])
        recycle()
        sums2 = qs
        sums2c = sb("sums2c", [P, NB, 3])
        with nc.Block() as block:
            @block.vector
            def _(v):
                nc.vector.tensor_copy(sums2[:, :, :], a2[:, :, 0:2 * A])
                nc.vector.tensor_copy(sums2c[:, :, :], a2[:, :, 2 * A:2 * A + 3])
        look_up("l2dst", "dst", lambda t, product: nc.vector.tensor_scalar(selfv[:, t, :], product, 1.0, None, ALU.mult))
        edge_weights("dst", "dst")

        def build3(link, t, h):
            nc.vector.tensor_tensor(rhs[h][:, :, 0:A], arow[h][:, :, :], bc(exe["dst"][:, t], [P, G, A]), ALU.mult)
            return nc.vector.tensor_scalar(flat(rhs[h][:, :, A:A + 1]), exe["dst"][:, t], 1.0, None, ALU.mult)

        a3 = aggregate("l2d", "dst", A + 1, build3, loads=[([arow[h][:, :, :] for h in range(2)], a_rows["dst"])])

        s_m2, s_e3 = sem("l2_sums"), sem("l2_node_exp")
        marks2 = []
        with nc.Block() as block:
            @block.vector
            def _(v):
                ch = Chain(v, s_m2)
                has, none, mn, e1, e2, loopv, edgev, tmp = (small[:, k, 0:NB] for k in range(8))
                hi, hj = node_vals[:, :, 0], node_vals[:, :, 1]
                ch.link(nc.vector.tensor_tensor(loopv, hi, hj, ALU.add))
                ch.link(nc.vector.scalar_tensor_tensor(out=loopv, in0=loopv, scalar=0.05, in1=loopv, op0=ALU.mult, op1=ALU.max))
                ch.link(nc.vector.tensor_scalar(none, cnt["src"][:, 0:NB], 0.0, None, ALU.is_equal))
                ch.link(nc.vector.tensor_tensor(mn, loopv, none, ALU.mult))
                ch.link(nc.vector.tensor_tensor(mn, mn, sums2c[:, :, 2], ALU.add))
                ch.link(nc.vector.tensor_tensor(e1, loopv, mn, ALU.subtract))
                marks2.append(ch.k)
                v.wait_ge(s_e3, 1)
                ch.link(nc.vector.tensor_tensor(e2, sums2c[:, :, 0], e1, ALU.add))
                ch.link(nc.vector.tensor_scalar(tmp, cnt["src"][:, 0:NB], 1.0, None, ALU.add))
                ch.link(nc.vector.tensor_tensor(e2, e2, tmp, ALU.mult))
                ch.link(nc.vector.reciprocal(e2, e2))
                ch.link(nc.vector.tensor_tensor(wide[:, :, 0:A], nodes2[:, :, 0:A], bc(e1, [P, NB, A]), ALU.mult))
                ch.link(nc.vector.tensor_tensor(wide[:, :, 0:A], wide[:, :, 0:A], sums2[:, :, 0:A], ALU.add))
                ch.link(nc.vector.tensor_tensor(wide[:, :, 0:A], wide[:, :, 0:A], bc(e2, [P, NB, A]), ALU.mult))
                ch.link(nc.vector.tensor_tensor(edgev, sums2c[:, :, 1], a3[:, :, A], ALU.add))
                ch.link(nc.vector.tensor_scalar(edgev, edgev, 1e-30, None, ALU.max))
                ch.link(nc.vector.tensor_tensor(tmp, cnt["src"][:, 0:NB], cnt["dst"][:, 0:NB], ALU.add))
                ch.link(nc.vector.tensor_scalar(tmp, tmp, 1.0, None, ALU.max))
                ch.link(nc.vector.tensor_tensor(edgev, edgev, tmp, ALU.mult))
                ch.link(nc.vector.reciprocal(edgev, edgev))
                ch.link(nc.vector.tensor_tensor(wide[:, :, A:2 * A], a3[:, :, 0:A], sums2[:, :, A:2 * A], ALU.add))
                ch.link(nc.vector.tensor_tensor(sums2[:, :, 0:A], wide[:, :, A:2 * A], bc(edgev, [P, NB, A]), ALU.mult))

            @block.scalar
            def _(act):
                act.wait_ge(s_m2, marks2[0])
                nc.scalar.activation(small[:, 3, 0:NB], small[:, 3, 0:NB], ACT.Exp).then_inc(s_e3, 1)

        node_products("l2e", lambda b: sums2[:, b, 0:A], A, wedgeT[:, :],
                      lambda b, product: nc.vector.tensor_copy(wide[:, b, A:2 * A], product))

        def update2(link):
            link(nc.vector.scalar_tensor_tensor(out=wide, in0=wide, scalar=0.05, in1=wide, op0=ALU.mult, op1=ALU.max))

        layer_norm("l2", update2)

        recycle()

        s_x3, s_mk = sem("x_table_written"), sem("kinds_marked")
        with nc.Block() as block:
            @block.sync
            def _(sp):
                sp.dma_start(x_table.rearrange("(b p) d -> p b d", p=P), xs[:, :, :]).then_inc(s_x3, 16)
                sp.wait_ge(s_x3, 16)

            @block.vector
            def _(v):
                nc.vector.tensor_scalar(slot_tmp[0][:, :], e3[:, :], 0.0, None, ALU.is_gt)
                nc.vector.tensor_scalar(slot_tmp[1][:, :], e3[:, :], 0.0, None, ALU.is_le).then_inc(s_mk, 1)
                v.wait_ge(s_mk, 1)
                nc.vector.tensor_tensor(slot_tmp[0][:, :], slot_tmp[0][:, :], l3w[0][:, :], ALU.mult)
                nc.vector.tensor_tensor(slot_tmp[1][:, :], slot_tmp[1][:, :], l3w[1][:, :], ALU.mult)

        def build4(link, t, h):
            for k in range(2):
                nc.vector.tensor_tensor(rhs[h][:, :, k * D:(k + 1) * D], grow[h][:, :, 0:D], bc(slot_tmp[k][:, t], [P, G, D]),
                                        ALU.mult)
            nc.vector.tensor_scalar(flat(rhs[h][:, :, 2 * D:2 * D + 1]), l3w[0][:, t], 1.0, None, ALU.mult)
            return nc.vector.tensor_scalar(flat(rhs[h][:, :, 2 * D + 1:2 * D + 2]), l3w[1][:, t], 1.0, None, ALU.mult)

        a4 = aggregate("l3", "dst", 2 * D + 2, build4, table_ap=x_table, index=other["dst"], width=D)
        s_q = sem("l3_divided")
        with nc.Block() as block:
            @block.vector
            def _(v):
                ch = Chain(v, s_q)
                for k in range(2):
                    r = small[:, k, 0:NB]
                    ch.link(nc.vector.tensor_scalar(r, a4[:, :, 2 * D + k], 1e-30, None, ALU.max))
                    ch.link(nc.vector.reciprocal(r, r))
                    ch.link(nc.vector.tensor_tensor(a4[:, :, k * D:(k + 1) * D], a4[:, :, k * D:(k + 1) * D],
                                                    bc(r, [P, NB, D]), ALU.mult))
        node_products("l3self", lambda b: xs[:, b, :], D, w3[:, 0, :],
                      lambda b, product: nc.vector.tensor_tensor(wide[:, b, :], product, b3[:, 0, :], ALU.add))
        for k in range(2):
            def take3(b, product, k=k):
                nc.vector.tensor_tensor(wide[:, b, :], wide[:, b, :], product, ALU.add)
                return nc.vector.tensor_scalar(nout[:, b % 2, 0:1], dinv[:, b:b + 1], 1.0, None, ALU.mult)
            node_products(f"l3n{k}", lambda b, k=k: a4[:, b, k * D:(k + 1) * D], D, w3[:, 1 + k, :],
                          lambda b, product: nc.vector.tensor_tensor(wide[:, b, :], wide[:, b, :], product, ALU.add))

        def update3(link):
            for k in range(2):
                link(nc.vector.tensor_tensor(wide, wide, bc(b3[:, 1 + k:2 + k, :], [P, NB, D]), ALU.add))

        layer_norm("l3", update3)
        s_out = sem("output_written")
        with nc.Block() as block:
            @block.sync
            def _(sp):
                full = (NB - 1) * P
                sp.dma_start(out[0:full, :].rearrange("(b p) d -> p b d", p=P), xs[:, 0:NB - 1, :]).then_inc(s_out, 16)
                sp.dma_start(out[full:N, :], xs[0:N - full, NB - 1, :]).then_inc(s_out, 16)
                sp.wait_ge(s_out, 32)


def kernel(**inputs):
    import numpy as np
    import concourse.bacc as bacc
    from concourse.bass_utils import run_bass_kernel_spmd as run

    a = {k: np.asarray(v) for k, v in inputs.items()}
    keys = np.full((2, EROWS), NPAD, np.int32)
    keys[0, :E] = a["dst"]
    keys[1, :E] = a["src"]
    arrays = {
        "x": a["x"],
        "keys": keys.reshape(2, P, ET),
        "edge_pair": np.ascontiguousarray(np.stack([a["src"], a["dst"]], axis=1)),
        "edge_attr": np.concatenate([a["edge_attr_64"], a["edge_attr_32"]], axis=1),
        "node_vec": a["node_vec"],
        "Wqkv": np.ascontiguousarray(np.concatenate([a["L0_gnn_Wq"], a["L0_gnn_Wk"], a["L0_gnn_Wv"]], axis=0).T),
        "WeT": np.ascontiguousarray(a["L0_gnn_We"].T),
        "L1_kernel": a["L1_gnn_kernel"],
        "L1_bias": a["L1_gnn_bias"],
        "W_node": a["L2_gnn_W_node"],
        "W_nodeT": np.ascontiguousarray(a["L2_gnn_W_node"].T),
        "W_edge": a["L2_gnn_W_edge"],
        "W_edgeT": np.ascontiguousarray(a["L2_gnn_W_edge"].T),
        "a_node": a["L2_gnn_a_node"],
        "a_edge": a["L2_gnn_a_edge"],
        "L3_W": np.stack([a["L3_gnn_W_self"], a["L3_gnn_W_homo"], a["L3_gnn_W_hete"]]),
        "L3_b": np.stack([a["L3_gnn_b_self"], a["L3_gnn_b_homo"], a["L3_gnn_b_hete"]]),
    }
    nc = bacc.Bacc("TRN2", target_bir_lowering=False, num_devices=1)
    aps = [nc.dram_tensor(f"in_{k}", v.shape, mybir.dt.from_np(v.dtype), kind="ExternalInput").ap() for k, v in arrays.items()]
    out = nc.dram_tensor("out", (N, D), F32, kind="ExternalOutput").ap()
    gnn_program(nc, *aps, out)
    got = run(nc, [{f"in_{k}": v for k, v in arrays.items()}], core_ids=[0])
    return got.results[0]["out"]
```

```python
from contextlib import ExitStack

import concourse.bass as bass
from concourse import mybir

F32 = mybir.dt.float32
I32 = mybir.dt.int32
BF16 = mybir.dt.bfloat16
F16 = mybir.dt.float16
ALU = mybir.AluOpType
ACT = mybir.ActivationFunctionType
AX_X = mybir.AxisListType.X
DVE_ONLY = (mybir.EngineType.DVE,)
PE_ONLY = (mybir.EngineType.PE,)

P = 128
N = 3125
D = 128
E = 53125
H, C = 8, 16
FE32, FE64 = 32, 64
NB = -(-N // P)
NPAD = NB * P
ET = -(-E // (8 * P)) * 8
EROWS = P * ET
T = -(-(E // P + NB) // 8) * 8
NH = NB + 1
ROW = FE64 + FE32 + 2
C_SRC, C_DST = FE64 + FE32, FE64 + FE32 + 1
KVW = 2 * D + 1
G = 4
SR = T // 4
SL = 4 * P
BIG = 3.0e38
NOWHERE = 60000.0
EPS = 1e-5
WN = 68


def wait(eng, sem, value):
    if isinstance(value, int) and value <= 0:
        return
    eng.wait_ge(sem, value)


def hold(eng, sem, value, passed):
    if isinstance(value, int):
        wait(eng, sem, value)
        return
    eng.wait_ge(sem, value)
    eng.sem_inc(passed, 1)


def loop(eng, count, body, last_too=False):
    body(0)
    with eng.Fori(1, count - 1 if last_too else count) as i:
        body(i)
    if last_too:
        body(count - 1)


class Chain:

    def __init__(self, eng, sem):
        self.eng, self.sem, self.per, self.k, self.i, self.base = eng, sem, 0, 0, 0, 0

    def start(self, i):
        if not (isinstance(i, int) and i == 0) and not self.per:
            self.per = self.k
        self.i, self.k = i, 0

    def link(self, ins):
        ins.then_inc(self.sem, 1)
        self.k += 1
        at = self.i * self.per + self.k if self.per else self.k
        self.eng.wait_ge(self.sem, at)


def gnn_program(nc, x, keys, edge_pair, edge_attr, node_vec, Wqkv, WeT, L1_kernel, L1_bias, W_node,
                W_nodeT, W_edge, W_edgeT, a_node, a_edge, L3_W, L3_b, out):
    ctx = ExitStack()
    with ctx:
        def sb(name, shape, dt=F32):
            return ctx.enter_context(nc.sbuf_tensor(name, shape, dt))

        stage_sems = []

        def lasting_sem(name):
            return ctx.enter_context(nc.semaphore(name))

        def sem(name):
            stage_sems.append(nc.alloc_semaphore(name=name))
            return stage_sems[-1]

        def recycle():
            with nc.Block() as block:
                @block.gpsimd
                def _(g):
                    nc.clear_and_free_semaphores(stage_sems)
                    for s in passed.values():
                        g.sem_clear(s)
            stage_sems.clear()

        def dram(name, shape):
            return nc.dram_tensor(name, shape, F32).ap()

        banks = ctx.enter_context(nc.psum_tensor("banks", [P, 8 * 512], F32))
        ps = [banks[:, i * 512:(i + 1) * 512] for i in range(8)]

        edge_table = dram("edge_table", (E, ROW))
        kv_table = dram("kv_table", (NPAD, KVW))
        y_table = dram("y_table", (NPAD, D))
        n_table = dram("n_table", (NPAD, WN))
        z_table = dram("z_table", (2 * NPAD, D))
        v_rows = dram("v_rows", (T // G, P, G * D))
        a_rows = {o: dram(f"a_rows_{o}", (T // G, P, G * FE64)) for o in ("dst", "src")}
        h_rows = dram("h_rows", (T // G, P, G * FE64))

        diff = sb("diff", [P, P])
        ident = sb("ident", [P, P])
        ident16 = sb("ident16", [P, P], BF16)
        iota0 = sb("iota0", [P, P])
        iota0h = sb("iota0h", [P, P], BF16)
        iota1 = sb("iota1", [P, P])
        iotaT = sb("iotaT", [P, T])
        iotaTh = sb("iotaTh", [P, T], F16)
        ones = sb("ones", [P, P])
        zeros = sb("zeros", [P, P])
        after = sb("after", [P, P])
        upto = sb("upto", [P, P])
        down1 = sb("down1", [P, P])
        up1 = sb("up1", [P, P])

        wqkv = sb("wqkv", [P, 3 * D])
        we_bd = sb("we_bd", [P, G * H])
        w1 = sb("w1", [P, D])
        b1 = sb("b1", [P, D])
        wn = sb("wn", [P, WN])
        wnode = sb("wnode", [FE64, D])
        wedge = sb("wedge", [FE64, FE64])
        wedgeT = sb("wedgeT", [FE64, FE64])
        avec = sb("avec", [FE64, 4])
        a_rep = sb("a_rep", [FE64, P])
        wge = sb("wge", [P, FE64])
        w3 = sb("w3", [P, 3, D])
        b3 = sb("b3", [P, 3, D])

        xs = sb("xs", [P, NB, D])
        nv = sb("nv", [P, NB])
        acc = sb("acc", [P, 5700])
        sums = acc[:, 0:NB * D].rearrange("p (b d) -> p b d", b=NB)
        side = acc[:, NB * D:NB * (D + 16)].rearrange("p (b c) -> p b c", b=NB)
        q16 = sb("q16", [P, NB, 3, D], BF16)
        NV = 6
        node_vals = sb("node_vals", [P, NB, NV])
        node_vals16 = sb("node_vals16", [P, NB, 3, NV], BF16)
        cnt = {o: sb(f"cnt_{o}", [P, NH]) for o in ("dst", "src")}
        gmax = {o: sb(f"gmax_{o}", [P, NB]) for o in ("dst", "src")}
        small = sb("small", [P, 8, NH])
        smalli = sb("smalli", [P, NH], I32)
        xt = sb("xt", [P, G, P])
        nout = sb("nout", [P, 2, KVW])

        eidx = {o: sb(f"eidx_{o}", [P, T], I32) for o in ("dst", "src")}
        valid = {o: sb(f"valid_{o}", [P, T]) for o in ("dst", "src")}
        lo1 = {o: sb(f"lo1_{o}", [P, T]) for o in ("dst", "src")}
        node = {o: sb(f"node_{o}", [P, T]) for o in ("dst", "src")}
        other = {o: sb(f"other_{o}", [P, T], I32) for o in ("dst", "src")}
        bid = {o: sb(f"bid_{o}", [1, T], I32) for o in ("dst", "src")}
        is_last = {o: sb(f"last_{o}", [P, T]) for o in ("dst", "src")}
        ge = {o: sb(f"ge_{o}", [P, T]) for o in ("dst", "src")}
        exe = {o: sb(f"exe_{o}", [P, T]) for o in ("dst", "src")}
        gm_slot = sb("gm_slot", [P, T])
        KD = H + 2
        S = sb("S", [P, T, KD])
        self_src, self_dst = S[:, :, 0:4], S[:, :, 4:8]
        slot_tmp = [sb(f"slot_tmp{i}", [P, T]) for i in range(4)]
        l3w = [sb(f"l3w{k}", [P, T]) for k in range(2)]
        dinv = sb("dinv", [P, NB])

        work = sb("work", [P, NH * (ET + 1)])
        table = work[:, :].rearrange("p (h t) -> p h t", h=NH)
        wide = work[:, 0:NB * D].rearrange("p (b d) -> p b d", b=NB)
        scan = [work[0:SR, k * SL:(k + 1) * SL] for k in range(6)]
        free = [exe["dst"], exe["src"], is_last["dst"], is_last["src"], gm_slot, slot_tmp[1], slot_tmp[2]]
        key_lo, key_hi, keyi, keyt, pos, num_hi, num_lo = (f[:, 0:ET] for f in free)
        key = {"lo": key_lo, "hi": key_hi}
        keyi, keyt, number = keyi.bitcast(I32), keyt.bitcast(I32), slot_tmp[3][:, 0:ET].bitcast(I32)
        slot_num = slot_tmp[0]
        cols_s = sb("cols_s", [P, 3, 12])
        rows_s = work[0:12, 17 * SL:18 * SL].rearrange("r (k n) -> r k n", k=4)

        taken = [0]

        def carve(words, dt, width, at=None):
            a = taken[0] if at is None else at
            taken[0] = a + words
            part = acc[:, a:a + words]
            return (part if dt == F32 else part.bitcast(dt)).rearrange("p (g n) -> p g n", n=width)

        big16 = [carve(G * T // 2, BF16, T) for _ in range(2)]
        sohT = [carve(G * P, F32, P) for _ in range(4)]
        so16 = [carve(G * P // 2, BF16, P) for _ in range(2)]
        ssame = [carve(G * P // 2, BF16, P) for _ in range(2)]
        hi16 = [carve(G * NH // 2, BF16, NH) for _ in range(4)]
        sprod = carve(G * NH, F32, NH)
        sohT16 = [carve(G * P // 2, BF16, P) for _ in range(2)]
        dist = [sohT[0], sohT[3]]
        minus_plo = sohT[1].rearrange("p g n -> p (g n)")[:, 0:ET]
        minus_num = sohT[2].rearrange("p g n -> p (g n)")[:, 0:ET]
        taken[0] = NB * (D + 16)
        oh_d = [carve(G * P, F32, P) for _ in range(2)]
        rhs_d = [carve(G * FE64, F32, FE64) for _ in range(2)]
        arow_d = [carve(G * FE64, F32, FE64) for _ in range(2)]
        taken[0] = NB * (D + 16)
        ohT_d = [carve(G * P, F32, P) for _ in range(2)]
        oh16_d = [work[:, (12 + h) * SL:(12 + h) * SL + G * P // 2].bitcast(BF16).rearrange("p (g n) -> p g n", g=G)
                  for h in range(2)]

        oh = [sb(f"oh{h}", [P, G, P]) for h in range(2)]
        both = [sb(f"both{h}", [P, 3 * G * P // 2]) for h in range(2)]
        rhs, ohT = ([r[:, 0:G * P].rearrange("p (g n) -> p g n", g=G) for r in both] for _ in range(2))
        oh16 = [r[:, G * P:].bitcast(BF16).rearrange("p (g n) -> p g n", g=G) for r in both]
        sides = [sb(f"sides{h}", [P, G, 16]) for h in range(2)]
        prod = [sb(f"prod{h}", [P, G, P]) for h in range(2)]
        bias = [sb(f"bias{h}", [P, G * H]) for h in range(2)]
        stage = [sb(f"stage{h}", [P, G], I32) for h in range(2)]
        erow = [sb(f"erow{h}", [P, G, ROW]) for h in range(2)]
        arow = [e[:, :, 0:FE64] for e in erow]
        grow = [sb(f"grow{h}", [P, G, KVW]) for h in range(2)]
        efeat = [sb(f"efeat{h}", [P, G * FE32]) for h in range(2)]
        tiny = [sb(f"tiny{h}", [P, 1, G * H]) for h in range(2)]
        tinyi = [sb(f"tinyi{h}", [P, G], I32) for h in range(2)]

        passed = {e: lasting_sem(f"passed_{e}") for e in ("act", "pool", "dve", "pe")}
        landed = [lasting_sem(f"gather_landed{i}") for i in range(2 * G)]
        rounds = [0]

        s_w, s_c, s_cd, s_wp = sem("weights_loaded"), sem("iotas_ready"), sem("consts_chain"), sem("wfold_done")
        s_t = sem("edge_table_written")
        s_xz = sem("x_cleared")
        with nc.Block() as block:
            @block.sync
            def _(sp):
                sp.wait_ge(s_xz, 1)
                full = (NB - 1) * P
                sp.dma_start(xs[:, 0:NB - 1, :], x[0:full, :].rearrange("(b p) d -> p b d", p=P)).then_inc(s_w, 16)
                sp.dma_start(xs[0:N - full, NB - 1, :], x[full:N, :]).then_inc(s_w, 16)
                with nc.allow_non_contiguous_dma(reason="node_vec into node layout"):
                    sp.dma_start(nv[:, 0:NB - 1], node_vec[0:full].rearrange("(b p) -> p b", p=P)).then_inc(s_w, 16)
                    sp.dma_start(nv[0:N - full, NB - 1:NB], node_vec[full:N].rearrange("(p o) -> p o", o=1)).then_inc(s_w, 16)
                sp.dma_start(wqkv[:, :], Wqkv).then_inc(s_w, 16)
                for j in range(G):
                    sp.dma_start(we_bd[j * FE32:(j + 1) * FE32, j * H:(j + 1) * H], WeT).then_inc(s_w, 16)
                sp.dma_start(w1[:, :], L1_kernel).then_inc(s_w, 16)
                sp.dma_start(b1[:, :], L1_bias[None, :].to_broadcast([P, D])).then_inc(s_w, 16)
                sp.dma_start(wnode[:, :], W_node).then_inc(s_w, 16)
                sp.dma_start(wn[:, 0:FE64], W_nodeT).then_inc(s_w, 16)
                sp.dma_start(wedge[:, :], W_edge).then_inc(s_w, 16)
                sp.dma_start(wedgeT[:, :], W_edgeT).then_inc(s_w, 16)
                with nc.allow_non_contiguous_dma(reason="attention vectors as columns"):
                    sp.dma_start(avec[:, 0:2], a_node.rearrange("(a d) -> d a", a=2)).then_inc(s_w, 16)
                    sp.dma_start(avec[:, 2:4], a_edge.rearrange("(a d) -> d a", a=2)).then_inc(s_w, 16)
                sp.dma_start(w3[:, :, :], L3_W.rearrange("m p d -> p m d")).then_inc(s_w, 16)
                for j in range(3):
                    sp.dma_start(b3[:, j, :], L3_b[j:j + 1, :].to_broadcast([P, D])).then_inc(s_w, 16)
                sp.wait_ge(s_w, 16 * 21)

            @block.gpsimd
            def _(g):
                nc.gpsimd.iota(diff[:, :], [[1, P]], base=0, channel_multiplier=-1,
                               allow_small_or_imprecise_dtypes=True).then_inc(s_c, 1)
                nc.gpsimd.iota(iota0[:, :], [[1, P]], base=0, channel_multiplier=0,
                               allow_small_or_imprecise_dtypes=True).then_inc(s_c, 1)
                nc.gpsimd.iota(iotaT[:, :], [[1, T]], base=0, channel_multiplier=0,
                               allow_small_or_imprecise_dtypes=True).then_inc(s_c, 1)
                nc.gpsimd.iota(number[:, :], [[1, ET]], base=1, channel_multiplier=ET).then_inc(s_c, 1)

            @block.vector
            def _(v):
                nc.vector.memset(we_bd[:, :], 0.0)
                nc.vector.memset(nv[:, :], 0.0)
                nc.vector.memset(wn[:, :], 0.0)
                nc.vector.memset(xs[:, :, :], 0.0).then_inc(s_xz, 1)
                v.wait_ge(s_c, 4)
                nc.vector.memset(ones[:, :], 1.0)
                nc.vector.memset(zeros[:, :], 0.0)
                for to, op, at in ((ident, ALU.is_equal, 0.0), (ident16, ALU.is_equal, 0.0), (after, ALU.is_gt, 0.0),
                                   (upto, ALU.is_ge, 0.0), (down1, ALU.is_equal, 1.0), (up1, ALU.is_equal, -1.0)):
                    nc.vector.tensor_scalar(to[:, :], diff[:, :], at, None, op)
                nc.vector.tensor_scalar(iota0h[:, :], iota0[:, :], 0.0, None, ALU.add)
                nc.vector.tensor_scalar(iota1[:, :], iota0[:, :], 1.0, None, ALU.add)
                nc.vector.tensor_scalar(iotaTh[:, :], iotaT[:, :], 0.0, None, ALU.add)
                ch = Chain(v, s_cd)
                ch.link(nc.vector.tensor_scalar(keyt[:, :], number[:, :], 8, None, ALU.arith_shift_right))
                nc.vector.tensor_copy(num_hi[:, :], keyt[:, :])
                ch.link(nc.vector.tensor_scalar(keyi[:, :], number[:, :], 255, None, ALU.bitwise_and))
                nc.vector.tensor_copy(num_lo[:, :], keyi[:, :])
                v.wait_ge(s_w, 16 * 21)
                ch.link(nc.vector.tensor_copy(a_rep[:, :], avec[:, 3:4].to_broadcast([FE64, P])))
                v.wait_ge(s_wp, 2)
                nc.vector.tensor_copy(wge[:, :], ps[0][:, 0:FE64])
                nc.vector.tensor_copy(wn[:, 64:65], ps[1][:, 1:2])
                nc.vector.tensor_copy(wn[:, 65:66], ps[1][:, 0:1])
                nc.vector.tensor_copy(wn[:, 66:67], ps[1][:, 2:3])

            @block.tensor
            def _(pe):
                pe.wait_ge(s_cd, 3)
                nc.tensor.matmul(ps[0][:, 0:FE64], a_rep[:, :], wedge[:, :], start=True, stop=True).then_inc(s_wp, 1)
                nc.tensor.matmul(ps[1][:, 0:4], wnode[:, :], avec[:, :], start=True, stop=True).then_inc(s_wp, 1)

        def run(*parts):
            turns = (parts[0][2] - parts[0][1]) // parts[0][3]
            assert all((last - first) == turns * ratio for _, first, last, ratio in parts)

            def engine_program(engine, eng):
                mine = [(p[engine], *rest) for p, *rest in parts if engine in p]

                slots = max(len(p["step"]) * ratio for p, _, _, ratio in mine) if mine else 0

                def turn(k):
                    for q in range(slots):
                        for program, first, _, ratio in mine:
                            phases = program["step"]
                            m = len(phases) * ratio
                            for c in range(q * m // slots, (q + 1) * m // slots):
                                phases[c % len(phases)](eng, k * ratio + (first + c // len(phases)))
                for program, first, _, _ in mine:
                    if first == 0 and "begin" in program:
                        program["begin"](eng)
                turn(0)
                if turns > 2:
                    with eng.Fori(1, turns - 1) as k:
                        turn(k)
                if turns > 1:
                    turn(turns - 1)
                for program, _, last, _ in mine:
                    if last == program["steps"] and "end" in program:
                        program["end"](eng)

            used = {e for p, *_ in parts for e in p}
            with nc.Block() as block:
                if "sync" in used:
                    @block.sync
                    def _(sp):
                        engine_program("sync", sp)
                if "pool" in used:
                    @block.gpsimd
                    def _(g):
                        engine_program("pool", g)
                if "vector" in used:
                    @block.vector
                    def _(v):
                        engine_program("vector", v)
                if "scalar" in used:
                    @block.scalar
                    def _(act):
                        engine_program("scalar", act)
                if "tensor" in used:
                    @block.tensor
                    def _(pe):
                        engine_program("tensor", pe)

        ESTEPS = ET // (2 * G)

        def keys_and_histogram(o, which):
            s_k, s_ch = sem(f"{o}_keys_loaded"), sem(f"{o}_key_chain")
            s_oh, s_hd, s_hc = sem(f"{o}_hist_onehots"), sem(f"{o}_hist_done"), sem(f"{o}_hist_copied")

            def load(sp):
                sp.dma_start(keyi[:, :], keys[which]).then_inc(s_k, 16)
                if o == "dst":
                    sp.dma_start(edge_table[:, 0:FE64 + FE32], edge_attr).then_inc(s_t, 16)
                    sp.dma_start(edge_table[:, C_SRC:C_SRC + 2].bitcast(I32), edge_pair).then_inc(s_t, 16)

            def split(v):
                ch = Chain(v, s_ch)
                v.wait_ge(s_k, 16)
                ch.link(nc.vector.tensor_scalar(keyt[:, :], keyi[:, :], 7, None, ALU.arith_shift_right))
                ch.link(nc.vector.tensor_copy(key["hi"][:, :], keyt[:, :]))
                ch.link(nc.vector.tensor_scalar(keyt[:, :], keyi[:, :], P - 1, None, ALU.bitwise_and))
                ch.link(nc.vector.tensor_copy(key["lo"][:, :], keyt[:, :]))
                nc.vector.memset(table[:, :, 0:1], 0.0)

            def onehots(v, i):
                for h in range(2):
                    t0 = i * (2 * G) + h * G
                    wait(v, s_hd, i * 2 + (h - 1))
                    nc.vector.tensor_tensor(so16[h][:, :, :], iota0[:, None, :].to_broadcast([P, G, P]),
                                            key["lo"][:, bass.ds(t0, G)].to_broadcast([P, G, P]), ALU.is_equal)
                    nc.vector.tensor_tensor(hi16[h][:, :, :], iota0[:, None, 0:NH].to_broadcast([P, G, NH]),
                                            key["hi"][:, bass.ds(t0, G)].to_broadcast([P, G, NH]),
                                            ALU.is_equal).then_inc(s_oh, 1)

            def count(pe, i):
                for h in range(2):
                    pe.wait_ge(s_oh, i * 2 + (h + 1))
                    wait(pe, s_hc, i * 2 + (h - 1))
                    for j in range(G):
                        last = nc.tensor.matmul(ps[6 + h][:, j * NH:(j + 1) * NH], so16[h][:, j, :],
                                                hi16[h][:, j, :], start=True, stop=True)
                    last.then_inc(s_hd, 1)

            def keep(act, i):
                for h in range(2):
                    hold(act, s_hd, i * 2 + (h + 1), passed["act"])
                    nc.scalar.copy(table[:, :, bass.ds(i * (2 * G) + (h * G + 1), G)],
                                   ps[6 + h][:, 0:G * NH].rearrange("p (g n) -> p n g", g=G)).then_inc(s_hc, 1)

            return {"sync": {"begin": load, "step": [lambda sp, i: None], "steps": ESTEPS},
                    "vector": {"begin": split, "step": [onehots], "steps": ESTEPS},
                    "tensor": {"step": [count], "steps": ESTEPS},
                    "scalar": {"step": [keep], "steps": ESTEPS}}

        def key_starts(o):
            s_v, s_p = sem(f"{o}_starts_chain"), sem(f"{o}_starts_products")
            total, tiles, ends, start, base = (small[:, k, :] for k in range(5))
            endc = small[0:NB, 5, 0:2]
            with nc.Block() as block:
                @block.vector
                def _(v):
                    ch = Chain(v, s_v)
                    ch.link(nc.vector.tensor_reduce(out=cnt[o][:, :], in_=table[:, :, 1:ET + 1], axis=AX_X, op=ALU.add))
                    v.wait_ge(s_p, 3)
                    ch.link(nc.vector.tensor_scalar(total, ps[0][:, 0:NH], float(P - 1), None, ALU.add))
                    ch.link(nc.vector.tensor_copy(smalli[:, :], total))
                    ch.link(nc.vector.tensor_scalar(smalli[:, :], smalli[:, :], 7, None, ALU.arith_shift_right))
                    ch.link(nc.vector.tensor_copy(tiles, smalli[:, :]))
                    ch.link(nc.vector.tensor_tensor_scan(ends, ones[:, 0:NH], tiles, 0.0, ALU.mult, ALU.add))
                    ch.link(nc.vector.tensor_tensor(start, ends, tiles, ALU.subtract))
                    ch.link(nc.vector.scalar_tensor_tensor(out=base, in0=start, scalar=float(P), in1=ps[1][:, 0:NH],
                                                           op0=ALU.mult, op1=ALU.add))
                    ch.link(nc.vector.memset(small[:, 4, NB:NH], NOWHERE))
                    ch.link(nc.vector.tensor_scalar(endc[:, 0:1], ps[2][0:NB, 0:1], float(P - 1), None, ALU.add))
                    ch.link(nc.vector.tensor_copy(smalli[0:NB, 0:1], endc[:, 0:1]))
                    ch.link(nc.vector.tensor_scalar(smalli[0:NB, 0:1], smalli[0:NB, 0:1], 7, None, ALU.arith_shift_right))
                    ch.link(nc.vector.tensor_copy(endc[:, 0:1], smalli[0:NB, 0:1]))
                    v.wait_ge(s_p, 4)
                    ch.link(nc.vector.tensor_copy(endc[:, 1:2], ps[3][0:NB, 0:1]))
                    ch.link(nc.vector.tensor_scalar(slot_num[0:NB, :], iotaT[0:NB, :], endc[:, 1:2], None, ALU.is_ge))
                    v.wait_ge(s_p, 5)
                    ch.link(nc.vector.tensor_scalar(bid[o][0:1, :], ps[4][0:1, 0:T], float(NB - 1), None, ALU.min))
                    for b in range(NH):
                        nc.vector.tensor_tensor_scan(table[:, b, :], ones[:, 0:1].to_broadcast([P, ET + 1]), table[:, b, :],
                                                     small[:, 4, b:b + 1], ALU.mult, ALU.add)

                @block.tensor
                def _(pe):
                    pe.wait_ge(s_v, 1)
                    nc.tensor.matmul(ps[0][:, 0:NH], ones[:, :], cnt[o][:, :], start=True, stop=True).then_inc(s_p, 1)
                    nc.tensor.matmul(ps[1][:, 0:NH], after[:, :], cnt[o][:, :], start=True, stop=True).then_inc(s_p, 1)
                    nc.tensor.matmul(ps[2][0:NB, 0:1], cnt[o][:, 0:NB], ones[:, 0:1], start=True, stop=True).then_inc(s_p, 1)
                    pe.wait_ge(s_v, 13)
                    nc.tensor.matmul(ps[3][0:NB, 0:1], upto[0:NB, 0:NB], endc[:, 0:1], start=True, stop=True).then_inc(s_p, 1)
                    pe.wait_ge(s_v, 15)
                    nc.tensor.matmul(ps[4][0:1, 0:T], ones[0:NB, 0:1], slot_num[0:NB, :], start=True,
                                     stop=True).then_inc(s_p, 1)

        def ranks(o):
            s_oh, s_td, s_tc = sem(f"{o}_rank_onehots"), sem(f"{o}_transposed"), sem(f"{o}_transposed_copied")
            s_sd, s_su, s_gd, s_pr, s_ps = (sem(f"{o}_same_done"), sem(f"{o}_same_masked"), sem(f"{o}_rank_done"),
                                            sem(f"{o}_rank_picked"), sem(f"{o}_slots_written"))
            steps, last_n = ET // (4 * G), ET // G - 1

            def dve_onehots(v, n, k):
                wait(v, s_td, n - 1)
                wait(v, s_ps, n - 3)
                nc.vector.tensor_tensor(so16[k % 2][:, :, :], iota0[:, None, :].to_broadcast([P, G, P]),
                                        key["lo"][:, bass.ds(n * G, G)].to_broadcast([P, G, P]), ALU.is_equal)
                nc.vector.tensor_tensor(hi16[k][:, :, :], iota0[:, None, 0:NH].to_broadcast([P, G, NH]),
                                        key["hi"][:, bass.ds(n * G, G)].to_broadcast([P, G, NH]),
                                        ALU.is_equal).then_inc(s_oh, 1)

            def dve_mask(v, n, k):
                v.wait_ge(s_sd, n + 1)
                wait(v, s_gd, n - 1)
                nc.vector.tensor_tensor(ssame[k % 2][:, :, :], ps[6 + k % 2][:, :].rearrange("p (g n) -> p g n", g=G),
                                        after[:, None, :].to_broadcast([P, G, P]), ALU.mult).then_inc(s_su, 1)

            def dve_pick(v, n, k):
                v.wait_ge(s_gd, n + 1)
                wait(v, s_ps, n)
                nc.vector.tensor_tensor(sprod[:, :, :], rank_bank(k).rearrange("p (g n) -> p g n", g=G),
                                        hi16[k][:, :, :], ALU.mult).then_inc(s_pr, 1)
                v.wait_ge(s_pr, n + 1)
                nc.vector.tensor_reduce(out=pos[:, bass.ds(n * G, G)], in_=sprod[:, :, :], axis=AX_X,
                                        op=ALU.add).then_inc(s_ps, 1)

            def rank_bank(k):
                return ps[3][:, 0:G * NH]

            def turned(k):
                return ps[2][:, 0:256].bitcast(BF16)

            def pe_transpose(pe, n, k):
                pe.wait_ge(s_oh, n + 1)
                wait(pe, s_tc, n)
                for j in range(G):
                    last = nc.tensor.transpose(turned(k)[:, j * P:(j + 1) * P], so16[k % 2][:, j, :], ident16[:, :])
                last.then_inc(s_td, 1)

            def pe_same(pe, n, k):
                pe.wait_ge(s_tc, n + 1)
                wait(pe, s_su, n - 1)
                for j in range(G):
                    last = nc.tensor.matmul(ps[6 + k % 2][:, j * P:(j + 1) * P], sohT16[k % 2][:, j, :], sohT16[k % 2][:, j, :],
                                            start=True, stop=True)
                last.then_inc(s_sd, 1)

            def pe_rank(pe, n, k):
                pe.wait_ge(s_su, n + 1)
                wait(pe, s_pr, n)
                for j in range(G):
                    to = rank_bank(k)[:, j * NH:(j + 1) * NH]
                    nc.tensor.matmul(to, sohT[k][:, j, :], table[:, :, bass.ds(n * G + j, 1)]
                                     .rearrange("p h t -> p (h t)"), start=True, stop=False)
                    last = nc.tensor.matmul(to, ssame[k % 2][:, j, :], hi16[k][:, j, :], start=False, stop=True)
                last.then_inc(s_gd, 1)

            def staggered(eng, i, stages):
                for k in range(4):
                    for lag, stage in stages:
                        if isinstance(i, int) and 4 * i + k - lag < 0:
                            continue
                        stage(eng, i * 4 + (k - lag), (k - lag) % 4)

            def drained(eng, stages):
                for newest in range(last_n + 1, last_n + 1 + max(lag for lag, _ in stages)):
                    for lag, stage in stages:
                        if newest - lag <= last_n:
                            stage(eng, newest - lag, (newest - lag) % 4)

            def copy_out(act, i):
                for k in range(4):
                    n = i * 4 + k
                    act.wait_ge(s_td, n + 1)
                    wait(act, s_sd, n - 1)
                    nc.scalar.copy(sohT16[k % 2][:, :, :], turned(k)[:, 0:G * P].rearrange("p (g n) -> p g n", g=G))
                    wait(act, s_gd, n - 3)
                    nc.scalar.copy(sohT[k][:, :, :], turned(k)[:, 0:G * P].rearrange("p (g n) -> p g n", g=G)) \
                      .then_inc(s_tc, 1)

            dve = ((4, dve_pick), (2, dve_mask), (0, dve_onehots))
            pet = ((1, pe_same), (3, pe_rank), (0, pe_transpose))
            return {"vector": {"step": [lambda v, i: staggered(v, i, dve)], "end": lambda v: drained(v, dve), "steps": steps},
                    "tensor": {"step": [lambda pe, i: staggered(pe, i, pet)], "end": lambda pe: drained(pe, pet), "steps": steps},
                    "scalar": {"step": [copy_out], "steps": steps}}

        def permutation(o):
            s_pc, s_in, s_pd = sem(f"{o}_slot_chain"), sem(f"{o}_scatter_ready"), sem(f"{o}_scatter_done")
            s_ab, s_lr = sem(f"{o}_distances"), sem(f"{o}_low_parts_ready")
            plo, phi = key["lo"], key["hi"]

            def split(v):
                ch = Chain(v, s_pc)
                ch.link(nc.vector.tensor_copy(keyi[:, :], pos[:, :]))
                ch.link(nc.vector.tensor_scalar(keyt[:, :], keyi[:, :], 7, None, ALU.arith_shift_right))
                ch.link(nc.vector.tensor_copy(phi[:, :], keyt[:, :]))
                ch.link(nc.vector.tensor_scalar(keyt[:, :], keyi[:, :], P - 1, None, ALU.bitwise_and))
                ch.link(nc.vector.tensor_copy(plo[:, :], keyt[:, :]))
                nc.vector.tensor_scalar(minus_plo, plo[:, :], -1.0, None, ALU.mult)
                ch.link(nc.vector.tensor_scalar(minus_num, num_lo[:, :], -1.0, None, ALU.mult))

            def low_parts(act, i):
                for h in range(2):
                    if isinstance(i, int) and i == 0 and h == 0:
                        act.wait_ge(s_pc, 6)
                    hold(act, s_lr, i * 2 + (h - 1), passed["act"])
                    for j in range(G):
                        t = bass.ds(i * (2 * G) + (h * G + j), 1)
                        nc.scalar.activation(dist[h][:, j, :], iota0[:, :], ACT.Abs, bias=minus_plo[:, t]).then_inc(s_ab, 1)
                    hold(act, s_ab, i * (2 * G) + (h * G + G), passed["act"])
                    if not (isinstance(i, int) and i == 0):
                        hold(act, s_pd, i * 2 + (h - 1), passed["act"])
                    for j in range(G):
                        t = bass.ds(i * (2 * G) + (h * G + j), 1)
                        last = nc.scalar.activation(ssame[h][:, j, :], dist[h][:, j, :], ACT.Relu, bias=num_lo[:, t],
                                                    scale=minus_num[:, t])
                    last.then_inc(s_lr, 1)

            def onehots(v, i):
                for h in range(2):
                    wait(v, s_pd, i * 2 + (h - 1))
                    for j in range(G):
                        t = bass.ds(i * (2 * G) + (h * G + j), 1)
                        nc.vector.tensor_scalar(so16[h][:, j, :], iota0h[:, :], plo[:, t], num_hi[:, t],
                                                ALU.is_equal, ALU.mult)
                        last = nc.vector.tensor_scalar(big16[h][:, j, :], iotaTh[:, :], phi[:, t], None, ALU.is_equal)
                    last.then_inc(s_in, 1)

            def finish(v):
                v.wait_ge(s_pd, ET // G)
                nc.vector.tensor_copy(slot_num[:, :], ps[7][:, 0:T]).then_inc(s_pc, 1)
                v.wait_ge(s_pc, 7)
                nc.vector.scalar_tensor_tensor(out=slot_num[:, :], in0=ps[6][:, 0:T], scalar=256.0, in1=slot_num[:, :],
                                               op0=ALU.mult, op1=ALU.add).then_inc(s_pc, 1)
                v.wait_ge(s_pc, 8)
                nc.vector.tensor_scalar(valid[o][:, :], slot_num[:, :], 1.0, None, ALU.is_ge)
                nc.vector.tensor_scalar(eidx[o][:, :], slot_num[:, :], -1.0, 0.0, ALU.add, ALU.max)

            def scatter(pe, i):
                for h in range(2):
                    pe.wait_ge(s_in, i * 2 + (h + 1))
                    pe.wait_ge(s_lr, i * 2 + (h + 1))
                    for j in range(G):
                        first = isinstance(i, int) and i == 0 and h == 0 and j == 0
                        final = isinstance(i, int) and i == ESTEPS - 1 and h == 1 and j == G - 1
                        nc.tensor.matmul(ps[6][:, 0:T], so16[h][:, j, :], big16[h][:, j, :], start=first, stop=final)
                        last = nc.tensor.matmul(ps[7][:, 0:T], ssame[h][:, j, :], big16[h][:, j, :], start=first,
                                                stop=final)
                    last.then_inc(s_pd, 1)

            return {"vector": {"begin": split, "step": [onehots], "end": finish, "steps": ESTEPS},
                    "scalar": {"step": [low_parts], "steps": ESTEPS},
                    "tensor": {"step": [scatter], "steps": ESTEPS}}

        def gather(to, table_ap, index, slot):
            nc.gpsimd.indirect_dma_start(to, None, table_ap, bass.IndirectOffsetOnAxis(ap=index, axis=0)) \
              .then_inc(landed[slot], 16)

        def stored_group(rows, i, h):
            return rows[bass.ds(i * 2 + h, 1), :, :].rearrange("o p (g c) -> p (o g) c", g=G)

        def wait_landed(eng, h, value, alone=None):
            for j in range(G):
                if alone is not None:
                    hold(eng, landed[h * G + j], value, alone)
                else:
                    eng.wait_ge(landed[h * G + j], value)

        def block_ids(o, t0):
            _, vals = nc.values_load_multi_w_load_instructions(
                bid[o][0:1, bass.ds(t0, G)], engines=PE_ONLY, min_val=0, max_val=NB - 1,
                skip_runtime_bounds_check_because="clamped to the last block when it was made")
            return vals

        STEPS = T // (2 * G)

        def edge_rows(o):
            full = o == "dst"
            own_col, other_col = (C_DST, C_SRC) if full else (C_SRC, C_DST)
            s_st, s_used, s_as = sem(f"{o}_staged"), sem(f"{o}_rows_used"), [sem(f"{o}_attr_stored{h}") for h in range(2)]
            s_ch = sem(f"{o}_rows_chain")
            s_oh, s_pt, s_at, s_pq = (sem(f"{o}_rows_onehots"), sem(f"{o}_rows_transposed"), sem(f"{o}_rows_copied"),
                                      sem(f"{o}_rows_products"))
            s_vs = [sem(f"{o}_v_stored{h}") for h in range(2)]
            s_ef, s_pb, s_bc = sem(f"{o}_features_packed"), sem(f"{o}_bias_product"), sem(f"{o}_bias_copied")
            base = 16 * rounds[0]
            per = 2 if full else 1
            rounds[0] += per * STEPS
            chain = []

            rohT = [r[:, 0:G * P // 2].bitcast(BF16).rearrange("p (g n) -> p g n", g=G) for r in both]

            def features(h):
                return ps[h][:, 256:256 + P], ps[h][:, 256 + P:256 + P + G * H]

            def pool(g, i):
                for h in range(2):
                    hold(g, s_used, i * 2 + (h - 1), passed["pool"])
                    hold(g, s_as[h], i * 16, passed["pool"])
                    if full:
                        hold(g, s_vs[h], i * 16, passed["pool"])
                    nc.gpsimd.tensor_copy(stage[h][:, :], eidx[o][:, bass.ds(i * (2 * G) + h * G, G)]).then_inc(s_st, 1)
                    hold(g, s_st, i * 2 + (h + 1), passed["pool"])
                    for j in range(G):
                        gather(erow[h][:, j, :], edge_table, stage[h][:, j:j + 1], h * G + j)
                if full:
                    for h in range(2):
                        wait_landed(g, h, i * 32 + (base + 16), passed["pool"])
                        for j in range(G):
                            gather(grow[h][:, j, :], kv_table, erow[h][:, j, C_SRC:C_SRC + 1].bitcast(I32), h * G + j)

            def store(sp, i):
                for h in range(2):
                    wait_landed(sp, h, i * (16 * per) + (base + 16))
                    sp.dma_start(stored_group(a_rows[o], i, h), erow[h][:, :, 0:FE64]).then_inc(s_as[h], 16)
                if full:
                    for h in range(2):
                        wait_landed(sp, h, i * (16 * per) + (base + 32))
                        sp.dma_start(stored_group(v_rows, i, h), grow[h][:, :, D:2 * D]).then_inc(s_vs[h], 16)

            def stored(sp):
                for h in range(2):
                    sp.wait_ge(s_as[h], 16 * STEPS)
                    if full:
                        sp.wait_ge(s_vs[h], 16 * STEPS)

            def vector_edges(v, i):
                if not chain:
                    chain.append(Chain(v, s_ch))
                ch = chain[0]
                ch.start(i)
                for h in range(2):
                    t = bass.ds(i * (2 * G) + h * G, G)
                    wait_landed(v, h, i * (16 * per) + (base + 16))
                    rows = erow[h]
                    own = rows[:, :, own_col:own_col + 1].bitcast(I32).rearrange("p g o -> p (g o)")
                    oth = rows[:, :, other_col:other_col + 1].bitcast(I32).rearrange("p g o -> p (g o)")
                    ch.link(nc.vector.tensor_scalar(tinyi[h][:, :], own, P - 1, None, ALU.bitwise_and))
                    nc.vector.tensor_scalar(other[o][:, t], oth, 0.0, None, ALU.add)
                    ch.link(nc.vector.scalar_tensor_tensor(out=lo1[o][:, t], in0=tinyi[h][:, :], scalar=1.0,
                                                           in1=valid[o][:, t], op0=ALU.add, op1=ALU.mult))
                    nc.vector.scalar_tensor_tensor(out=node[o][:, t], in0=own, scalar=1.0, in1=valid[o][:, t],
                                                   op0=ALU.add, op1=ALU.mult)
                    if full:
                        nc.vector.tensor_tensor(oh16[h][:, :, :], iota1[:, None, :].to_broadcast([P, G, P]),
                                                lo1[o][:, t].to_broadcast([P, G, P]), ALU.is_equal).then_inc(s_oh, 1)
                    ch.link(nc.vector.tensor_tensor(prod[h][:, :, 0:FE64], rows[:, :, 0:FE64],
                                                    wge[:, None, :].to_broadcast([P, G, FE64]), ALU.mult))
                    last = nc.vector.tensor_reduce(out=ge[o][:, t], in_=prod[h][:, :, 0:FE64], axis=AX_X, op=ALU.add)
                    if full:
                        ch.link(last)
                    else:
                        last.then_inc(s_used, 1)

            def vector_scores(v, i):
                ch = chain[0]
                if full:
                    for h in range(2):
                        t = bass.ds(i * (2 * G) + h * G, G)
                        wait_landed(v, h, i * 32 + (base + 32))
                        v.wait_ge(s_pq, i * 2 + (h + 1))
                        v.wait_ge(s_bc, i * 2 + (h + 1))
                        ch.link(nc.vector.tensor_tensor(prod[h][:, :, :], ps[4 + h][:, :].rearrange("p (g n) -> p g n", g=G),
                                                        grow[h][:, :, 0:D], ALU.mult))
                        qk = tiny[h][:, 0, :]
                        ch.link(nc.vector.tensor_reduce(out=qk, in_=prod[h][:, :, :].rearrange("p g (h c) -> p (g h) c", c=C),
                                                        axis=AX_X, op=ALU.add))
                        nvc = grow[h][:, :, 2 * D:KVW].rearrange("p g o -> p (g o)")
                        nc.vector.tensor_scalar(S[:, t, H:H + 1].rearrange("p g o -> p (g o)"), nvc, 1.0, None, ALU.mult)
                        nc.vector.scalar_tensor_tensor(
                            out=S[:, t, 0:H], in0=qk.rearrange("p (g h) -> p g h", h=H), scalar=1.0 / C ** 0.5,
                            in1=bias[h][:, :].rearrange("p (g h) -> p g h", h=H),
                            op0=ALU.mult, op1=ALU.add).then_inc(s_used, 1)

            def scalar(act, i):
                for h in range(2):
                    wait_landed(act, h, i * 32 + (base + 16))
                    wait(act, s_pq, i * 2 + (h - 1))
                    nc.scalar.copy(efeat[h][:, :].rearrange("p (g f) -> p g f", g=G),
                                   erow[h][:, :, FE64:FE64 + FE32]).then_inc(s_ef, 1)
                    act.wait_ge(s_pt, i * 2 + (h + 1))
                    nc.scalar.copy(xt[:, h, :], features(h)[0])
                    nc.scalar.copy(rohT[h], ps[h][:, 0:256].bitcast(BF16)[:, 0:G * P]
                                   .rearrange("p (g n) -> p g n", g=G)).then_inc(s_at, 1)

            def scalar_bias(act, i):
                for h in range(2):
                    act.wait_ge(s_pb, i * 2 + (h + 1))
                    wait(act, s_used, i * 2 + (h - 1))
                    nc.scalar.copy(bias[h][:, :], features(h)[1]).then_inc(s_bc, 1)

            def tensor(pe, i):
                for h in range(2):
                    pe.wait_ge(s_ef, i * 2 + (h + 1))
                    wait(pe, s_bc, i * 2 + (h - 1))
                    nc.tensor.transpose(features(h)[0], efeat[h][:, :], ident[:, :])
                    pe.wait_ge(s_oh, i * 2 + (h + 1))
                    for j in range(G):
                        last = nc.tensor.transpose(ps[h][:, 0:256].bitcast(BF16)[:, j * P:(j + 1) * P],
                                                   oh16[h][:, j, :], ident16[:, :])
                    last.then_inc(s_pt, 1)

            def tensor_products(pe, i):
                for h in range(2):
                    blocks = block_ids(o, i * (2 * G) + h * G)
                    pe.wait_ge(s_at, i * 2 + (h + 1))
                    nc.tensor.matmul(features(h)[1], xt[:, h, :], we_bd[:, :], start=True, stop=True).then_inc(s_pb, 1)
                    wait(pe, s_used, i * 2 + (h - 1))
                    for j in range(G):
                        for k in range(3):
                            last = nc.tensor.matmul(ps[4 + h][:, j * P:(j + 1) * P], rohT[h][:, j, :],
                                                    q16[:, bass.ds(blocks[j], 1), k, :].rearrange("p o d -> p (o d)"),
                                                    start=k == 0, stop=k == 2)
                    last.then_inc(s_pq, 1)

            program = {"pool": {"step": [pool], "steps": STEPS}, "sync": {"step": [store], "end": stored, "steps": STEPS},
                       "vector": {"step": [vector_edges, vector_scores] if full else [vector_edges], "steps": STEPS}}
            if full:
                program["scalar"] = {"step": [scalar, scalar_bias], "steps": STEPS}
                program["tensor"] = {"step": [tensor, tensor_products], "steps": STEPS}
            return program

        def segment_max(name, o, channels, flags):
            K = len(channels)
            s_t, s_c, s_v, s_m, s_b = (sem(f"{name}_{k}") for k in
                                       ("turned", "turned_copied", "scan_chain", "carries", "turned_back"))
            keys_s, keep_f, keep_b, pre_f, pre_b, last_s = (scan[k] for k in range(6))
            vals = [work[0:SR, (6 + c) * SL:(7 + c) * SL] for c in range(K)]
            ends, thru, enter = (cols_s[0:SR, k, :] for k in range(3))
            rows = [rows_s[0:K, k, 0:SR] for k in range(4)]
            HALF = 1.5e38

            with nc.Block() as block:
                marks = []

                @block.vector
                def _(v):
                    ch = Chain(v, s_v)

                    def link(ins):
                        ch.link(ins)
                    v.wait_ge(s_m, 1)
                    nc.vector.tensor_tensor(keep_f[:, 1:SL], keys_s[:, 1:SL], keys_s[:, 0:SL - 1], ALU.is_equal)
                    nc.vector.tensor_tensor(keep_f[:, 0:1], keys_s[:, 0:1], ps[0][0:SR, 0:1], ALU.is_equal)
                    nc.vector.tensor_tensor(keep_b[:, 0:SL - 1], keys_s[:, 0:SL - 1], keys_s[:, 1:SL], ALU.is_equal)
                    link(nc.vector.tensor_tensor(keep_b[:, SL - 1:SL], keys_s[:, SL - 1:SL], ps[0][0:SR, 1:2], ALU.is_equal))
                    if flags:
                        nc.vector.tensor_scalar(last_s, keep_b, -1.0, 1.0, ALU.mult, ALU.add)
                    nc.vector.tensor_tensor_scan(pre_f, ones[0:SR, 0:1].to_broadcast([SR, SL]), keep_f, 1.0, ALU.mult, ALU.min)
                    link(nc.vector.tensor_tensor_scan(pre_b[:, ::-1], ones[0:SR, 0:1].to_broadcast([SR, SL]), keep_b[:, ::-1],
                                                      1.0, ALU.mult, ALU.min))
                    for f in (keep_f, keep_b, pre_f, pre_b):
                        last = nc.vector.tensor_scalar(f, f, 2 * HALF, -HALF, ALU.mult, ALU.add)
                    link(last)
                    for back in (False, True):
                        keep, pre, edge = (keep_b, pre_b, 0) if back else (keep_f, pre_f, SL - 1)

                        def rev(ap, back=back):
                            return ap[:, ::-1] if back else ap
                        for c in range(K):
                            last = nc.vector.tensor_tensor_scan(rev(vals[c]), rev(keep), rev(vals[c]), -BIG, ALU.min, ALU.max)
                        link(last)
                        for c in range(K):
                            nc.vector.tensor_copy(ends[:, c:c + 1], vals[c][:, edge:edge + 1])
                        link(nc.vector.tensor_copy(thru[:, 0:K], pre[:, edge:edge + 1].to_broadcast([SR, K])))
                        marks.append(ch.k)
                        v.wait_ge(s_m, 2 + 2 * back)
                        nc.vector.tensor_copy(rows[0], ps[1][0:K, 0:SR])
                        link(nc.vector.tensor_copy(rows[1], ps[2][0:K, 0:SR]))
                        link(nc.vector.tensor_tensor_scan(rev(rows[2]), rev(rows[1]), rev(rows[0]), -BIG, ALU.min, ALU.max))
                        link(nc.vector.memset(rows[3], -HALF))
                        if back:
                            link(nc.vector.tensor_copy(rows[3][:, 0:SR - 1], rows[2][:, 1:SR]))
                        else:
                            link(nc.vector.tensor_copy(rows[3][:, 1:SR], rows[2][:, 0:SR - 1]))
                        marks.append(ch.k)
                        v.wait_ge(s_m, 3 + 2 * back)
                        link(nc.vector.tensor_copy(enter[:, 0:K], ps[3][0:SR, 0:K]))
                        for c in range(K):
                            last = nc.vector.scalar_tensor_tensor(out=vals[c], in0=pre, scalar=enter[:, c:c + 1], in1=vals[c],
                                                                  op0=ALU.min, op1=ALU.max)
                        link(last)
                    marks.append(ch.k)
                    n = 0
                    for done in ([lambda k, m: nc.vector.tensor_copy(is_last[o][:, k:T:4], m)] if flags else []) + \
                            [c[1] for c in channels]:
                        for k in range(4):
                            v.wait_ge(s_b, 4 * n + k + 1)
                            done(k, ps[(n % 2) * 4 + k][:, 0:SR]).then_inc(s_v, 1)
                        n += 1

                @block.scalar
                def _(act):
                    for n, dst in enumerate([keys_s] + vals):
                        for k in range(4):
                            act.wait_ge(s_t, 4 * n + k + 1)
                            nc.scalar.copy(dst[:, k * P:(k + 1) * P], ps[(n % 2) * 4 + k][0:SR, 0:P]).then_inc(s_c, 1)

                @block.tensor
                def _(pe):
                    for n, src in enumerate([node[o][:, :]] + [c[0] for c in channels]):
                        for k in range(4):
                            if n >= 2:
                                pe.wait_ge(s_c, 4 * (n - 2) + k + 1)
                            nc.tensor.transpose(ps[(n % 2) * 4 + k][0:SR, 0:P], src[:, k:T:4], ident[:, :]).then_inc(s_t, 1)
                    pe.wait_ge(s_c, 4 * (K + 1))
                    nc.tensor.matmul(ps[0][0:SR, 0:1], down1[0:SR, 0:SR], keys_s[:, SL - 1:SL], start=True, stop=True)
                    nc.tensor.matmul(ps[0][0:SR, 1:2], up1[0:SR, 0:SR], keys_s[:, 0:1], start=True, stop=True).then_inc(s_m, 1)
                    for back in range(2):
                        pe.wait_ge(s_v, marks[2 * back])
                        nc.tensor.transpose(ps[1][0:K, 0:SR], ends[:, 0:K], ident[0:SR, 0:SR])
                        nc.tensor.transpose(ps[2][0:K, 0:SR], thru[:, 0:K], ident[0:SR, 0:SR]).then_inc(s_m, 1)
                        pe.wait_ge(s_v, marks[2 * back + 1])
                        nc.tensor.transpose(ps[3][0:SR, 0:K], rows[3], ident[0:K, 0:K]).then_inc(s_m, 1)
                    pe.wait_ge(s_v, marks[4])
                    for n, src in enumerate(([last_s] if flags else []) + vals):
                        for k in range(4):
                            if n >= 2:
                                pe.wait_ge(s_v, marks[4] + 4 * (n - 2) + k + 1)
                            nc.tensor.transpose(ps[(n % 2) * 4 + k][:, 0:SR], src[:, k * P:(k + 1) * P],
                                                ident[0:SR, 0:SR]).then_inc(s_b, 1)

        MAIN = 512 // P
        SIDE = 16

        def clear_sums():
            with nc.Block() as block:
                @block.tensor
                def _(pe):
                    for b in range(8):
                        nc.tensor.matmul(ps[b][:, :], zeros[:, :], xs[:, 0:MAIN, :].rearrange("p b d -> p (b d)"),
                                         start=True, stop=True)

        def take_sums():
            def copy_bank(copy, b):
                n = min(MAIN, NB - b * MAIN)
                copy(sums[:, b * MAIN:b * MAIN + n, :], ps[b][:, 0:n * P].rearrange("p (b c) -> p b c", c=P))

            with nc.Block() as block:
                @block.vector
                def _(v):
                    nc.vector.tensor_copy(side[:, :, :], ps[7][:, 0:NB * SIDE].rearrange("p (b c) -> p b c", b=NB))
                    for b in range(4):
                        copy_bank(nc.vector.tensor_copy, b)

                @block.scalar
                def _(act):
                    for b in range(4, 7):
                        copy_bank(nc.scalar.copy, b)

        def aggregate(name, o, build, buf, cols, side_cols, col0=0, side0=0, loads=(), load_queue="scalar", side16=None, table_ap=None, index=None, width=0):
            s_st, s_z = sem(f"{name}_staged"), sem(f"{name}_chain")
            s_in, s_rd, s_pd = [sem(f"{name}_loaded{h}") for h in range(2)], sem(f"{name}_rhs_ready"), sem(f"{name}_summed")
            base = 16 * rounds[0]
            chain = []
            s_16 = sem(f"{name}_onehots16")
            oh_16 = [s_[:, :, :] for s_ in buf["oh16"]]

            def narrow(act, i):
                for h in range(2):
                    act.wait_ge(s_rd, i * 2 + (h + 1))
                    wait(act, s_pd, i * 2 + (h - 1))
                    nc.scalar.copy(oh_16[h], buf["oh"][h][:, :, :]).then_inc(s_16, 1)

            def load(act, i):
                for h in range(2):
                    wait(act, s_rd, i * 2 + (h - 1))
                    for to, rows in loads:
                        act.dma_start(to[h], stored_group(rows, i, h)).then_inc(s_in[h], 16)

            def pool(g, i):
                for h in range(2):
                    hold(g, s_rd, i * 2 + (h - 1), passed["pool"])
                    nc.gpsimd.tensor_copy(stage[h][:, :], index[:, bass.ds(i * (2 * G) + h * G, G)]).then_inc(s_st, 1)
                    hold(g, s_st, i * 2 + (h + 1), passed["pool"])
                    for j in range(G):
                        gather(grow[h][:, j, 0:width], table_ap, stage[h][:, j:j + 1], h * G + j)

            def vector(v, i):
                if not chain:
                    chain.append(Chain(v, s_z))
                chain[0].start(i)
                for h in range(2):
                    t = bass.ds(i * (2 * G) + h * G, G)
                    wait(v, s_pd, i * 2 + (h - 1))
                    nc.vector.tensor_tensor(buf["oh"][h][:, :, :], iota1[:, None, :].to_broadcast([P, G, P]),
                                            lo1[o][:, t].to_broadcast([P, G, P]), ALU.is_equal)
                    if loads:
                        v.wait_ge(s_in[h], i * (16 * len(loads)) + 16 * len(loads))
                    if table_ap is not None:
                        wait_landed(v, h, i * 16 + (base + 16))
                    build(chain[0].link, t, h).then_inc(s_rd, 1)

            def tensor(pe, i):
                for h in range(2):
                    blocks = block_ids(o, i * (2 * G) + h * G)
                    pe.wait_ge(s_rd, i * 2 + (h + 1))
                    if side16 is not None:
                        pe.wait_ge(s_16, i * 2 + (h + 1))
                    for j in range(G):
                        if side16 is not None:
                            nc.tensor.matmul(banks[:, bass.ds(blocks[j] * SIDE + (7 * 512 + side0), side_cols)],
                                             oh_16[h][:, j, :],
                                             side16[:, bass.ds(i * (2 * G) + (h * G + j), 1), :].rearrange("p o c -> p (o c)"),
                                             start=False, stop=True, skip_group_check=True)
                        elif side_cols:
                            nc.tensor.matmul(banks[:, bass.ds(blocks[j] * SIDE + (7 * 512 + side0), side_cols)],
                                             buf["oh"][h][:, j, :], buf["side"][h][:, j, 0:side_cols],
                                             start=False, stop=True, skip_group_check=True)
                        last = nc.tensor.matmul(banks[:, bass.ds(blocks[j] * P + col0, cols)], buf["oh"][h][:, j, :],
                                                buf["rhs"][h][:, j, 0:cols], start=False, stop=True, skip_group_check=True)
                    last.then_inc(s_pd, 1)

            program = {"vector": {"step": [vector], "steps": STEPS}, "tensor": {"step": [tensor], "steps": STEPS}}
            if loads:
                program[load_queue] = {"step": [load], "steps": STEPS}
            if side16 is not None:
                program["scalar"] = {"step": ([load] if loads and load_queue == "scalar" else []) + [narrow], "steps": STEPS}
            if table_ap is not None:
                program["pool"] = {"step": [pool], "steps": STEPS}
                rounds[0] += STEPS
            return program

        def look_up(name, o, out_vals, first_val, buf, table_ap=None, index=None, width=0, keep_rows=None, extra=None):
            s_st, s_oh, s_td, s_tc, s_pd, s_wr = (sem(f"{name}_{k}") for k in
                                                  ("staged", "onehots", "transposed", "copied", "looked_up", "written"))
            s_hs = [sem(f"{name}_stored{h}") for h in range(2)]
            base = 16 * rounds[0]
            half = buf["half"]

            def ohT16(h):
                return buf["ohT"][h][:, 0:G // 2, :].rearrange("p g n -> p (g n)").bitcast(BF16).rearrange("p (g n) -> p g n", g=G)

            def turned(h):
                return ps[2 * half + h][:, 0:256].bitcast(BF16)

            def pool(g, i):
                for h in range(2):
                    hold(g, s_wr, i * 2 + (h - 1), passed["pool"])
                    hold(g, s_hs[h], i * 16, passed["pool"])
                    nc.gpsimd.tensor_copy(stage[h][:, :], index[:, bass.ds(i * (2 * G) + h * G, G)]).then_inc(s_st, 1)
                    hold(g, s_st, i * 2 + (h + 1), passed["pool"])
                    for j in range(G):
                        gather(grow[h][:, j, 0:width], table_ap, stage[h][:, j:j + 1], h * G + j)

            def store(sp, i):
                for h in range(2):
                    wait_landed(sp, h, i * 16 + (base + 16))
                    sp.dma_start(stored_group(keep_rows, i, h), grow[h][:, :, 0:FE64]).then_inc(s_hs[h], 16)

            def stored(sp):
                for h in range(2):
                    sp.wait_ge(s_hs[h], 16 * STEPS)

            def vector(v, i):
                for h in range(2):
                    t = bass.ds(i * (2 * G) + h * G, G)
                    wait(v, s_td, i * 2 + (h - 1))
                    nc.vector.tensor_tensor(buf["oh16"][h][:, :, :], iota1[:, None, :].to_broadcast([P, G, P]),
                                            lo1[o][:, t].to_broadcast([P, G, P]), ALU.is_equal).then_inc(s_oh, 1)

            def vector_write(v, i):
                for h in range(2):
                    t = bass.ds(i * (2 * G) + h * G, G)
                    if table_ap is not None:
                        wait_landed(v, h, i * 16 + (base + 16))
                        extra(t, h)
                    v.wait_ge(s_pd, i * 2 + (h + 1))
                    picked = ps[4 + 2 * half + h][:, 0:3 * NV * G].rearrange("p (g s k) -> p g k s", g=G, s=3)
                    nc.vector.tensor_reduce(out=out_vals[:, t, :], in_=picked[:, :, first_val:first_val + 4, :], axis=AX_X,
                                            op=ALU.add).then_inc(s_wr, 1)

            def scalar(act, i):
                for h in range(2):
                    act.wait_ge(s_td, i * 2 + (h + 1))
                    wait(act, s_pd, i * 2 + (h - 1))
                    nc.scalar.copy(ohT16(h), turned(h)[:, 0:G * P].rearrange("p (g n) -> p g n", g=G)) \
                      .then_inc(s_tc, 1)

            def tensor(pe, i):
                for h in range(2):
                    pe.wait_ge(s_oh, i * 2 + (h + 1))
                    wait(pe, s_tc, i * 2 + (h - 1))
                    for j in range(G):
                        last = nc.tensor.transpose(turned(h)[:, j * P:(j + 1) * P], buf["oh16"][h][:, j, :], ident16[:, :])
                    last.then_inc(s_td, 1)

            def tensor_pick(pe, i):
                for h in range(2):
                    blocks = block_ids(o, i * (2 * G) + h * G)
                    pe.wait_ge(s_tc, i * 2 + (h + 1))
                    wait(pe, s_wr, i * 2 + (h - 1))
                    for j in range(G):
                        last = nc.tensor.matmul(ps[4 + 2 * half + h][:, 3 * NV * j:3 * NV * (j + 1)], ohT16(h)[:, j, :],
                                                node_vals16[:, bass.ds(blocks[j], 1), :, :].rearrange("p o s d -> p (o s d)"),
                                                start=True, stop=True)
                    last.then_inc(s_pd, 1)

            program = {"vector": {"step": [vector, vector_write], "steps": STEPS},
                       "scalar": {"step": [scalar], "steps": STEPS},
                       "tensor": {"step": [tensor, tensor_pick], "steps": STEPS}}
            if table_ap is not None:
                program["pool"] = {"step": [pool], "steps": STEPS}
                program["sync"] = {"step": [store], "end": stored, "steps": STEPS}
                rounds[0] += STEPS
            return program

        def split16(link, value, parts):
            for k, part in enumerate(parts):
                link(nc.vector.tensor_copy(part, value))
                if k < 2:
                    link(nc.vector.tensor_tensor(value, value, part, ALU.subtract))

        def node_products(name, source, width, weights, take, store=None, before=None, groups=None):
            s_b, s_t, s_c, s_p, s_k = (sem(f"{name}_{k}") for k in ("input", "transposed", "copied", "product", "taken"))
            s_s = [sem(f"{name}_stored{k}") for k in range(2)]
            with nc.Block() as block:
                @block.vector
                def _(v):
                    if before is not None:
                        before(Chain(v, s_b))
                    for b in range(NB):
                        v.wait_ge(s_p, b + 1)
                        if store is not None and b >= 2:
                            v.wait_ge(s_s[b % 2], 16 * (b // 2))
                        take(b, ps[4 + b % 4][:, 0:width]).then_inc(s_k, 1)

                @block.tensor
                def _(pe):
                    if before is not None:
                        pe.wait_ge(s_b, before.links)
                    for b in range(NB + 1):
                        if b < NB:
                            k = source(b).shape[-1]
                            if b >= 4:
                                pe.wait_ge(s_c, b - 3)
                            nc.tensor.transpose(ps[b % 4][0:k, 0:P], source(b), ident[:, :]).then_inc(s_t, 1)
                        if b:
                            pe.wait_ge(s_c, b)
                            if b > 4:
                                pe.wait_ge(s_k, b - 4)
                            nc.tensor.matmul(ps[4 + (b - 1) % 4][:, 0:width], xt[0:weights.shape[0], (b - 1) % 4, :], weights,
                                             start=True, stop=True).then_inc(s_p, 1)

                @block.scalar
                def _(act):
                    for b in range(NB):
                        k = source(b).shape[-1]
                        act.wait_ge(s_t, b + 1)
                        if b >= 4:
                            act.wait_ge(s_p, b - 3)
                        nc.scalar.copy(xt[0:k, b % 4, :], ps[b % 4][0:k, 0:P]).then_inc(s_c, 1)

                if store is not None:
                    @block.sync
                    def _(sp):
                        for b in range(NB):
                            sp.wait_ge(s_k, b + 1)
                            sp.dma_start(store[b * P:(b + 1) * P, :], nout[:, b % 2, 0:width if store is not kv_table else KVW]) \
                              .then_inc(s_s[b % 2], 16)
                        for k in range(2):
                            sp.wait_ge(s_s[k], 16 * ((NB + 1 - k) // 2))

        def bc(ap, shape):
            return ap.to_broadcast(shape)

        def layer_norm(name, update):
            s_v, s_r = sem(f"{name}_norm"), sem(f"{name}_root")
            marks = []
            with nc.Block() as block:
                @block.vector
                def _(v):
                    ch = Chain(v, s_v)
                    update(ch.link)
                    mean, var = small[:, 6, 0:NB], small[:, 7, 0:NB]
                    ch.link(nc.vector.tensor_tensor(xs[:, :, :], xs[:, :, :], wide, ALU.add))
                    ch.link(nc.vector.tensor_reduce(out=mean, in_=xs[:, :, :], axis=AX_X, op=ALU.add))
                    ch.link(nc.vector.tensor_scalar(mean, mean, 1.0 / D, None, ALU.mult))
                    ch.link(nc.vector.tensor_tensor(xs[:, :, :], xs[:, :, :], bc(mean, [P, NB, D]), ALU.subtract))
                    ch.link(nc.vector.tensor_tensor(wide, xs[:, :, :], xs[:, :, :], ALU.mult))
                    ch.link(nc.vector.tensor_reduce(out=var, in_=wide, axis=AX_X, op=ALU.add))
                    ch.link(nc.vector.tensor_scalar(var, var, 1.0 / D, EPS, ALU.mult, ALU.add))
                    marks.append(ch.k)
                    v.wait_ge(s_r, 1)
                    ch.link(nc.vector.reciprocal(var, var))
                    ch.link(nc.vector.tensor_tensor(xs[:, :, :], xs[:, :, :], bc(var, [P, NB, D]), ALU.mult))

                @block.scalar
                def _(act):
                    act.wait_ge(s_v, marks[0])
                    nc.scalar.activation(small[:, 7, 0:NB], small[:, 7, 0:NB], ACT.Sqrt).then_inc(s_r, 1)

        q_rest = S[:, :, :].rearrange("p t c -> p (t c)")[:, 0:NB * D].rearrange("p (b d) -> p b d", b=NB)

        def take_qkv(b, product):
            nc.vector.tensor_copy(q_rest[:, b, :], product[:, 0:D])
            nc.vector.tensor_copy(nout[:, b % 2, 2 * D:KVW], nv[:, b:b + 1])
            return nc.vector.tensor_copy(nout[:, b % 2, 0:2 * D], product[:, D:3 * D])

        def flat(ap):
            return ap.rearrange("p g o -> p (g o)")

        whole = {"oh": oh, "rhs": rhs, "side": sides, "oh16": oh16, "ohT": ohT, "half": 0}
        beside = {"oh": oh_d, "rhs": rhs_d, "side": None, "oh16": oh16_d, "ohT": ohT_d, "half": 1}

        node_products("qkv", lambda b: xs[:, b, :], 3 * D, wqkv[:, :], take_qkv, store=kv_table)
        s_qp = sem("q_parts")
        with nc.Block() as block:
            @block.vector
            def _(v):
                split16(Chain(v, s_qp).link, q_rest, [q16[:, :, k, :] for k in range(3)])
        run((keys_and_histogram("dst", 0), 0, ESTEPS, 1))
        key_starts("dst")
        run((ranks("dst"), 0, ESTEPS // 2, 1))
        run((permutation("dst"), 0, ESTEPS, 1))
        with nc.Block() as block:
            @block.gpsimd
            def _(g):
                g.wait_ge(s_t, 32)
        recycle()

        rows = edge_rows("dst")
        run((rows, 0, 13, 1), (keys_and_histogram("src", 1), 0, 52, 4))
        key_starts("src")
        run((rows, 13, 26, 1), (ranks("src"), 0, 26, 2))
        run((rows, 26, 52, 1), (permutation("src"), 0, 52, 2))
        run((rows, 52, STEPS, 1))
        recycle()

        s_l3 = sem("l3_logits")
        e3 = slot_tmp[3]
        with nc.Block() as block:
            @block.vector
            def _(v):
                ch = Chain(v, s_l3)
                e, minus = e3[:, :], slot_tmp[2][:, :]
                ch.link(nc.vector.tensor_copy(e, S[:, :, H]))
                ch.link(nc.vector.scalar_tensor_tensor(out=S[:, :, H], in0=e, scalar=0.2, in1=e, op0=ALU.mult, op1=ALU.max))
                ch.link(nc.vector.tensor_scalar(minus, e, -1.0, None, ALU.mult))
                ch.link(nc.vector.scalar_tensor_tensor(out=S[:, :, H + 1], in0=minus, scalar=0.2, in1=minus,
                                                       op0=ALU.mult, op1=ALU.max))

        def minus_max(c):
            return lambda k, m: nc.vector.tensor_tensor(S[:, k:T:4, c], S[:, k:T:4, c], m, ALU.subtract)

        def keep_max(to):
            return lambda k, m: nc.vector.tensor_copy(to[:, k:T:4], m)

        segment_max("dst", "dst", [(S[:, :, c], minus_max(c)) for c in range(KD)] + [(ge["dst"][:, :], keep_max(gm_slot))], True)
        s_x1 = sem("exp_done")
        with nc.Block() as block:
            @block.scalar
            def _(act):
                nc.scalar.activation(S[:, :, :], S[:, :, :], ACT.Exp).then_inc(s_x1, 1)

            @block.vector
            def _(v):
                v.wait_ge(s_x1, 1)
                for k in range(2):
                    nc.vector.tensor_copy(l3w[k][:, :], S[:, :, H + k])

        def build0(link, t, h):
            nc.vector.tensor_tensor(rhs[h][:, :, :].rearrange("p g (h c) -> p g h c", c=C),
                                    grow[h][:, :, 0:D].rearrange("p g (h c) -> p g h c", c=C),
                                    bc(S[:, t, 0:H], [P, G, H, C]), ALU.mult)
            nc.vector.tensor_scalar(sides[h][:, :, 0:KD], S[:, t, :], 1.0, None, ALU.mult)
            return nc.vector.tensor_tensor(flat(sides[h][:, :, KD:KD + 1]), gm_slot[:, t], is_last["dst"][:, t], ALU.mult)

        clear_sums()
        agg0 = aggregate("l0", "dst", build0, whole, D, KD + 1, loads=[([grow[h][:, :, 0:D] for h in range(2)], v_rows)])
        run((edge_rows("src"), 0, STEPS, 1), (agg0, 0, STEPS, 1))
        take_sums()

        def update0(link):
            den = prod[0][:, :, :].rearrange("p g n -> p (g n)")[:, 0:NB * KD].rearrange("p (b h) -> p b h", b=NB)
            link(nc.vector.tensor_copy(gmax["dst"][:, :], side[:, :, KD]))
            link(nc.vector.tensor_scalar(den, side[:, :, 0:KD], 1e-30, None, ALU.max))
            link(nc.vector.reciprocal(den, den))
            link(nc.vector.tensor_copy(node_vals[:, :, 4:6], den[:, :, H:KD]))
            link(nc.vector.tensor_tensor(wide.rearrange("p b (h c) -> p b h c", c=C),
                                         sums[:, :, :].rearrange("p b (h c) -> p b h c", c=C),
                                         bc(den[:, :, 0:H], [P, NB, H, C]), ALU.mult))

        layer_norm("l0", update0)
        recycle()

        s_d0, s_d1 = sem("degree_ready"), sem("degree_root")
        with nc.Block() as block:
            @block.vector
            def _(v):
                nc.vector.tensor_scalar(dinv[:, :], cnt["src"][:, 0:NB], 1.0, None, ALU.max).then_inc(s_d0, 1)
                v.wait_ge(s_d1, 1)
                nc.vector.reciprocal(dinv[:, :], dinv[:, :]).then_inc(s_d0, 1)
                nc.vector.tensor_scalar(small[:, 0, 0:NB], cnt["src"][:, 0:NB], 0.0, None, ALU.is_gt).then_inc(s_d0, 1)
                v.wait_ge(s_d0, 3)
                nc.vector.tensor_tensor(dinv[:, :], dinv[:, :], small[:, 0, 0:NB], ALU.mult)

            @block.scalar
            def _(act):
                act.wait_ge(s_d0, 1)
                nc.scalar.activation(dinv[:, :], dinv[:, :], ACT.Sqrt).then_inc(s_d1, 1)

        node_products("l1", lambda b: xs[:, b, :], D, w1[:, :],
                      lambda b, product: nc.vector.tensor_scalar(nout[:, b % 2, 0:D], product, dinv[:, b:b + 1], None, ALU.mult),
                      store=y_table)
        segment_max("src", "src", [(ge["src"][:, :], keep_max(gm_slot))], True)

        def build1(link, t, h):
            nc.vector.tensor_scalar(rhs[h][:, :, :], grow[h][:, :, 0:D], 1.0, None, ALU.mult)
            return nc.vector.tensor_tensor(flat(sides[h][:, :, 0:1]), gm_slot[:, t], is_last["src"][:, t], ALU.mult)

        clear_sums()
        run((aggregate("l1", "src", build1, whole, D, 1, table_ap=y_table, index=other["src"], width=D), 0, STEPS, 1))
        take_sums()

        def update1(link):
            link(nc.vector.tensor_copy(gmax["src"][:, :], side[:, :, 0]))
            link(nc.vector.tensor_tensor(wide, sums, bc(dinv[:, :], [P, NB, D]), ALU.mult))
            link(nc.vector.tensor_tensor(wide, wide, bc(b1[:, None, :], [P, NB, D]), ALU.add))
            link(nc.vector.tensor_scalar(wide, wide, 0.0, None, ALU.max))

        layer_norm("l1", update1)
        recycle()

        nodes2 = work[:, NB * D:NB * (D + WN)].rearrange("p (b c) -> p b c", b=NB)

        def take2(b, product):
            nc.vector.tensor_copy(nodes2[:, b, :], product)
            return nc.vector.tensor_copy(nout[:, b % 2, 0:WN], product)

        node_products("l2", lambda b: xs[:, b, :], WN, wn[:, :], take2, store=n_table)
        s_n2 = sem("node_values2")
        with nc.Block() as block:
            @block.vector
            def _(v):
                ch = Chain(v, s_n2)
                for k, col in enumerate((65, 64, 66)):
                    ch.link(nc.vector.tensor_copy(node_vals[:, :, k], nodes2[:, :, col]))
                for o in ("dst", "src"):
                    ch.link(nc.vector.tensor_scalar(small[:, 0, 0:NB], cnt[o][:, 0:NB], 0.0, -1e30, ALU.is_equal, ALU.mult))
                    ch.link(nc.vector.tensor_tensor(gmax[o][:, :], gmax[o][:, :], small[:, 0, 0:NB], ALU.add))
                m = small[:, 1, 0:NB]
                ch.link(nc.vector.tensor_tensor(m, gmax["dst"][:, :], gmax["src"][:, :], ALU.max))
                ch.link(nc.vector.tensor_tensor(m, m, node_vals[:, :, 2], ALU.add))
                ch.link(nc.vector.scalar_tensor_tensor(out=node_vals[:, :, 3], in0=m, scalar=0.05, in1=m,
                                                       op0=ALU.mult, op1=ALU.max))
                rest = prod[0][:, :, :].rearrange("p g n -> p (g n)")[:, 0:NB * NV].rearrange("p (b k) -> p b k", b=NB)
                ch.link(nc.vector.tensor_copy(rest, node_vals[:, :, :]))
                split16(ch.link, rest, [node_vals16[:, :, k, :] for k in range(3)])

        hj_slot = slot_tmp[0]

        def extra2(t, h):
            nc.vector.tensor_scalar(hj_slot[:, t], flat(grow[h][:, :, 64:65]), 1.0, None, ALU.mult)

        run((look_up("l2src", "src", self_src, 0, whole, table_ap=n_table, index=other["src"], width=WN, keep_rows=h_rows, extra=extra2), 0, STEPS, 1),
            (look_up("l2dst", "dst", self_dst, 2, beside), 0, STEPS, 1))

        s_e, s_f = sem("edge_arguments"), sem("edge_exp")
        with nc.Block() as block:
            @block.vector
            def _(v):
                ch = Chain(v, s_e)
                for o, he, m in (("src", self_src[:, :, 2], self_src[:, :, 3]), ("dst", self_dst[:, :, 0], self_dst[:, :, 1])):
                    w = exe[o][:, :]
                    ch.link(nc.vector.tensor_tensor(w, ge[o][:, :], he, ALU.add))
                    ch.link(nc.vector.scalar_tensor_tensor(out=w, in0=w, scalar=0.05, in1=w, op0=ALU.mult, op1=ALU.max))
                    ch.link(nc.vector.tensor_tensor(w, w, m, ALU.subtract))
                    ch.link(nc.vector.tensor_scalar(w, w, 0.0, None, ALU.min))
                nc.vector.tensor_tensor(slot_tmp[1][:, :], hj_slot[:, :], self_src[:, :, 1], ALU.max)

            @block.scalar
            def _(act):
                for n, o in enumerate(("src", "dst")):
                    act.wait_ge(s_e, 4 * (n + 1))
                    nc.scalar.activation(exe[o][:, :], exe[o][:, :], ACT.Exp).then_inc(s_f, 1)

        mslot, exn = slot_tmp[2], slot_tmp[1]
        kept2 = nodes2
        scan_end = (6 + 1) * SL
        assert scan_end <= NB * D + 384
        nodes2_kept = q16[:, :, :, :].rearrange("p b s d -> p (b s d)").bitcast(F32)[:, 0:NB * WN] \
            .rearrange("p (b c) -> p b c", b=NB)
        s_k2 = sem("node_rows_kept")
        with nc.Block() as block:
            @block.vector
            def _(v):
                nc.vector.tensor_copy(nodes2_kept, kept2)
        segment_max("l2", "src", [(exn[:, :], keep_max(mslot))], False)
        s_e2, s_f2 = sem("l2_arguments"), sem("l2_exp")
        with nc.Block() as block:
            @block.vector
            def _(v):
                ch = Chain(v, s_e2)
                m, w = mslot[:, :], exn[:, :]
                ch.link(nc.vector.tensor_tensor(m, m, self_src[:, :, 0], ALU.add))
                ch.link(nc.vector.scalar_tensor_tensor(out=m, in0=m, scalar=0.05, in1=m, op0=ALU.mult, op1=ALU.max))
                ch.link(nc.vector.tensor_tensor(w, hj_slot[:, :], self_src[:, :, 0], ALU.add))
                ch.link(nc.vector.scalar_tensor_tensor(out=w, in0=w, scalar=0.05, in1=w, op0=ALU.mult, op1=ALU.max))
                ch.link(nc.vector.tensor_tensor(w, w, m, ALU.subtract))
                ch.link(nc.vector.tensor_scalar(w, w, 0.0, None, ALU.min))
                ch.link(nc.vector.tensor_tensor(m, m, is_last["src"][:, :], ALU.mult))

            @block.scalar
            def _(act):
                act.wait_ge(s_e2, 6)
                nc.scalar.activation(exn[:, :], exn[:, :], ACT.Exp).then_inc(s_f2, 1)

        A = FE64

        def build2(link, t, h):
            nc.vector.tensor_tensor(rhs[h][:, :, 0:A], grow[h][:, :, 0:A], bc(exn[:, t], [P, G, A]), ALU.mult)
            return nc.vector.tensor_tensor(rhs[h][:, :, A:2 * A], arow[h][:, :, :], bc(exe["src"][:, t], [P, G, A]), ALU.mult)

        def build2d(link, t, h):
            return nc.vector.tensor_tensor(rhs_d[h][:, :, :], arow_d[h][:, :, :], bc(exe["dst"][:, t], [P, G, A]), ALU.mult)

        side_src = work[:, 0:T * 5].bitcast(BF16)[:, 0:T * 9].rearrange("p (t s c) -> p t s c", s=3, c=3)
        side_dst = work[:, T * 5:T * 7].bitcast(BF16)[:, 0:T * 3].rearrange("p (t s) -> p t s", s=3)
        s_sp = sem("side_parts")
        with nc.Block() as block:
            @block.vector
            def _(v):
                ch = Chain(v, s_sp)
                rest = slot_tmp[0][:, :]
                for c, value in enumerate((exn, exe["src"], mslot)):
                    ch.link(nc.vector.tensor_copy(rest, value[:, :]))
                    split16(ch.link, rest, [side_src[:, :, k, c] for k in range(3)])
                ch.link(nc.vector.tensor_copy(rest, exe["dst"][:, :]))
                split16(ch.link, rest, [side_dst[:, :, k] for k in range(3)])

        clear_sums()
        run((aggregate("l2s", "src", build2, whole, 2 * A, 9, side16=side_src.rearrange("p t s c -> p t (s c)"),
                       loads=[([grow[h][:, :, 0:A] for h in range(2)], h_rows), (arow, a_rows["src"])]), 0, STEPS, 1),
            (aggregate("l2d", "dst", build2d, beside, A, 3, col0=A, side0=9, side16=side_dst, loads=[(arow_d, a_rows["dst"])],
                       load_queue="sync"), 0, STEPS, 1))
        take_sums()
        recycle()

        s_m2, s_e3 = sem("l2_sums"), sem("l2_node_exp")
        marks2 = []
        with nc.Block() as block:
            @block.vector
            def _(v):
                ch = Chain(v, s_m2)
                ch.link(nc.vector.tensor_tensor(side[:, :, 0:3], side[:, :, 0:3], side[:, :, 3:6], ALU.add))
                ch.link(nc.vector.tensor_tensor(side[:, :, 0:3], side[:, :, 0:3], side[:, :, 6:9], ALU.add))
                for k in range(9, 12):
                    ch.link(nc.vector.tensor_tensor(side[:, :, 1], side[:, :, 1], side[:, :, k], ALU.add))
                none, mn, e1, e2, loopv, edgev, tmp = (small[:, k, 0:NB] for k in range(1, 8))
                hi, hj = node_vals[:, :, 0], node_vals[:, :, 1]
                ch.link(nc.vector.tensor_tensor(loopv, hi, hj, ALU.add))
                ch.link(nc.vector.scalar_tensor_tensor(out=loopv, in0=loopv, scalar=0.05, in1=loopv, op0=ALU.mult, op1=ALU.max))
                ch.link(nc.vector.tensor_scalar(none, cnt["src"][:, 0:NB], 0.0, None, ALU.is_equal))
                ch.link(nc.vector.tensor_tensor(mn, loopv, none, ALU.mult))
                ch.link(nc.vector.tensor_tensor(mn, mn, side[:, :, 2], ALU.add))
                ch.link(nc.vector.tensor_tensor(e1, loopv, mn, ALU.subtract))
                marks2.append(ch.k)
                v.wait_ge(s_e3, 1)
                ch.link(nc.vector.tensor_tensor(e2, side[:, :, 0], e1, ALU.add))
                ch.link(nc.vector.tensor_scalar(tmp, cnt["src"][:, 0:NB], 1.0, None, ALU.add))
                ch.link(nc.vector.tensor_tensor(e2, e2, tmp, ALU.mult))
                ch.link(nc.vector.reciprocal(e2, e2))
                ch.link(nc.vector.tensor_tensor(wide[:, :, 0:A], nodes2_kept[:, :, 0:A], bc(e1, [P, NB, A]), ALU.mult))
                ch.link(nc.vector.tensor_tensor(wide[:, :, 0:A], wide[:, :, 0:A], sums[:, :, 0:A], ALU.add))
                ch.link(nc.vector.tensor_tensor(wide[:, :, 0:A], wide[:, :, 0:A], bc(e2, [P, NB, A]), ALU.mult))
                ch.link(nc.vector.tensor_scalar(edgev, side[:, :, 1], 1e-30, None, ALU.max))
                ch.link(nc.vector.tensor_tensor(tmp, cnt["src"][:, 0:NB], cnt["dst"][:, 0:NB], ALU.add))
                ch.link(nc.vector.tensor_scalar(tmp, tmp, 1.0, None, ALU.max))
                ch.link(nc.vector.tensor_tensor(edgev, edgev, tmp, ALU.mult))
                ch.link(nc.vector.reciprocal(edgev, edgev))
                ch.link(nc.vector.tensor_tensor(sums[:, :, 0:A], sums[:, :, A:2 * A], bc(edgev, [P, NB, A]), ALU.mult))

            @block.scalar
            def _(act):
                act.wait_ge(s_m2, marks2[0])
                nc.scalar.activation(small[:, 3, 0:NB], small[:, 3, 0:NB], ACT.Exp).then_inc(s_e3, 1)

        node_products("l2e", lambda b: sums[:, b, 0:A], A, wedgeT[:, :],
                      lambda b, product: nc.vector.tensor_copy(wide[:, b, A:2 * A], product))

        def update2(link):
            link(nc.vector.scalar_tensor_tensor(out=wide, in0=wide, scalar=0.05, in1=wide, op0=ALU.mult, op1=ALU.max))

        layer_norm("l2", update2)

        def take3(b, product):
            return nc.vector.tensor_copy(nout[:, b % 2, 0:D], product)

        for k in range(2):
            node_products(f"l3z{k}", lambda b: xs[:, b, :], D, w3[:, 1 + k, :], take3, store=z_table[k * NPAD:(k + 1) * NPAD, :])
        s_mk = sem("kinds_marked")
        with nc.Block() as block:
            @block.vector
            def _(v):
                ch = Chain(v, s_mk)
                a, b, homo = slot_tmp[0][:, :], slot_tmp[1][:, :], slot_tmp[2][:, :]
                ch.link(nc.vector.tensor_tensor(a, l3w[0][:, :], self_dst[:, :, 2], ALU.mult))
                ch.link(nc.vector.tensor_tensor(b, l3w[1][:, :], self_dst[:, :, 3], ALU.mult))
                ch.link(nc.vector.scalar_tensor_tensor(out=a, in0=e3[:, :], scalar=0.0, in1=a, op0=ALU.is_gt, op1=ALU.mult))
                ch.link(nc.vector.scalar_tensor_tensor(out=b, in0=e3[:, :], scalar=0.0, in1=b, op0=ALU.is_le, op1=ALU.mult))
                ch.link(nc.vector.tensor_tensor(a, a, b, ALU.add))
                ch.link(nc.vector.tensor_scalar(homo, e3[:, :], 0.0, float(NPAD), ALU.is_le, ALU.mult))
                ch.link(nc.vector.tensor_tensor(other["dst"][:, :], other["dst"][:, :], homo, ALU.add))

        def build3(link, t, h):
            return nc.vector.tensor_tensor(rhs[h][:, :, :], grow[h][:, :, 0:D], bc(slot_tmp[0][:, t], [P, G, D]), ALU.mult)

        clear_sums()
        run((aggregate("l3", "dst", build3, whole, D, 0, table_ap=z_table, index=other["dst"], width=D), 0, STEPS, 1))
        take_sums()
        node_products("l3self", lambda b: xs[:, b, :], D, w3[:, 0, :],
                      lambda b, product: nc.vector.tensor_tensor(wide[:, b, :], product, sums[:, b, :], ALU.add))

        def update3(link):
            for k in range(3):
                link(nc.vector.tensor_tensor(wide, wide, bc(b3[:, k:k + 1, :], [P, NB, D]), ALU.add))

        layer_norm("l3", update3)
        s_out = sem("output_written")
        with nc.Block() as block:
            @block.sync
            def _(sp):
                full = (NB - 1) * P
                sp.dma_start(out[0:full, :].rearrange("(b p) d -> p b d", p=P), xs[:, 0:NB - 1, :]).then_inc(s_out, 16)
                sp.dma_start(out[full:N, :], xs[0:N - full, NB - 1, :]).then_inc(s_out, 16)
                sp.wait_ge(s_out, 32)


def kernel(**inputs):
    import numpy as np
    import concourse.bacc as bacc
    from concourse.bass_utils import run_bass_kernel_spmd as run

    a = {k: np.asarray(v) for k, v in inputs.items()}
    keys = np.full((2, EROWS), NPAD, np.int32)
    keys[0, :E] = a["dst"]
    keys[1, :E] = a["src"]
    arrays = {
        "x": a["x"],
        "keys": keys.reshape(2, P, ET),
        "edge_pair": np.ascontiguousarray(np.stack([a["src"], a["dst"]], axis=1)),
        "edge_attr": np.concatenate([a["edge_attr_64"], a["edge_attr_32"]], axis=1),
        "node_vec": a["node_vec"],
        "Wqkv": np.ascontiguousarray(np.concatenate([a["L0_gnn_Wq"], a["L0_gnn_Wk"], a["L0_gnn_Wv"]], axis=0).T),
        "WeT": np.ascontiguousarray(a["L0_gnn_We"].T),
        "L1_kernel": a["L1_gnn_kernel"],
        "L1_bias": a["L1_gnn_bias"],
        "W_node": a["L2_gnn_W_node"],
        "W_nodeT": np.ascontiguousarray(a["L2_gnn_W_node"].T),
        "W_edge": a["L2_gnn_W_edge"],
        "W_edgeT": np.ascontiguousarray(a["L2_gnn_W_edge"].T),
        "a_node": a["L2_gnn_a_node"],
        "a_edge": a["L2_gnn_a_edge"],
        "L3_W": np.stack([a["L3_gnn_W_self"], a["L3_gnn_W_homo"], a["L3_gnn_W_hete"]]),
        "L3_b": np.stack([a["L3_gnn_b_self"], a["L3_gnn_b_homo"], a["L3_gnn_b_hete"]]),
    }
    nc = bacc.Bacc("TRN2", target_bir_lowering=False, num_devices=1)
    aps = [nc.dram_tensor(f"in_{k}", v.shape, mybir.dt.from_np(v.dtype), kind="ExternalInput").ap() for k, v in arrays.items()]
    out = nc.dram_tensor("out", (N, D), F32, kind="ExternalOutput").ap()
    gnn_program(nc, *aps, out)
    got = run(nc, [{f"in_{k}": v for k, v in arrays.items()}], core_ids=[0])
    return got.results[0]["out"]
```
